# Optimizing a Trainium2 kernel written in Bass

```python
import numpy as np
import jax
import jax.numpy as jnp

def _softmax(x, axis=-1):
    return jax.nn.softmax(x, axis=axis)

def _gelu(x):
    return jax.nn.gelu(x, approximate=True)

def _silu(x):
    return jax.nn.silu(x)

def _sigmoid(x):
    return jax.nn.sigmoid(x)

def _layernorm(x, axis=-1, eps=1e-05):
    m = jnp.mean(x, axis=axis, keepdims=True)
    v = jnp.var(x, axis=axis, keepdims=True)
    return (x - m) / jnp.sqrt(v + eps)

def _scatter_add(tgt, idx, src, axis=0):
    return tgt.at[idx].add(src)

def _segment_sum(src, seg, n):
    return jax.ops.segment_sum(src, seg, n)
kernel_name = 'mk_adj_ffn_d1_adj_r2_0e735d'

def setup_inputs(seed: int=0):
    np.random.seed(seed)
    _w = jnp.asarray

    def _rec_inputs():
        import jax
        import jax.numpy as jnp
        _gk = jax.random.key(seed)
        x = -0.000125 + 0.9999 * jax.random.normal(jax.random.fold_in(_gk, 1), (32, 256, 128), jnp.float32)
        _a = jax.random.bernoulli(jax.random.fold_in(_gk, 2), 0.0078125, (256, 256))
        _a = jnp.logical_or(_a, jnp.swapaxes(_a, -1, -2))
        _a = jnp.logical_or(_a, jnp.eye(256, dtype=bool))
        _af = _a.astype(jnp.float32)
        _af = _af * jax.random.uniform(jax.random.fold_in(_gk, 3), (256, 256), jnp.float32, 0.05, 0.000488281)
        adj = _af
        return (x, adj)
    x, adj = _rec_inputs()

    def _L0_gnn_setup():
        import jax, jax.numpy as jnp
        import numpy as np
        B, T, D, H = (64, 1024, 128, 128)
        MAX_SKIP = 4

        def _lstm_last(Wih, Whh, bih, bhh, xs):
            N, _, Hd = xs.shape
            bias = bih + bhh

            def step(carry, x_t):
                h, c = carry
                g = x_t @ Wih.T + h @ Whh.T + bias
                i, f, gg, o = jnp.split(g, 4, axis=-1)
                c = jax.nn.sigmoid(f) * c + jax.nn.sigmoid(i) * jnp.tanh(gg)
                h = jax.nn.sigmoid(o) * jnp.tanh(c)
                return ((h, c), None)
            init = (jnp.zeros((N, Hd), xs.dtype), jnp.zeros((N, Hd), xs.dtype))
            (h_last, _), _ = jax.lax.scan(step, init, jnp.swapaxes(xs, 0, 1))
            return h_last
        key = jax.random.key(seed)
        ks = jax.random.split(key, 8)
        s = 0.05
        x = jax.random.normal(ks[0], (B, T, D), jnp.float32)
        adj = jax.random.uniform(ks[1], (T, T), jnp.float32) / T
        Wg0 = jax.random.normal(ks[2], (D, H), jnp.float32) * s
        bg0 = jnp.zeros((H,), jnp.float32)
        Wg1 = jax.random.normal(ks[3], (H, H), jnp.float32) * s
        bg1 = jnp.zeros((H,), jnp.float32)
        Wih = jax.random.normal(ks[4], (MAX_SKIP, 4 * H, H), jnp.float32) * s
        Whh = jax.random.normal(ks[5], (MAX_SKIP, 4 * H, H), jnp.float32) * s
        bih = jax.random.normal(ks[6], (MAX_SKIP, 4 * H), jnp.float32) * s
        bhh = jax.random.normal(ks[7], (MAX_SKIP, 4 * H), jnp.float32) * s
        return dict(x=x, adj=adj, Wg0=Wg0, bg0=bg0, Wg1=Wg1, bg1=bg1, Wih=Wih, Whh=Whh, bih=bih, bhh=bhh)
    _L0_gnn_all = _L0_gnn_setup()
    _L0_gnn_in = {k: v for k, v in _L0_gnn_all.items() if k in ('Wg0', 'bg0', 'Wg1', 'bg1', 'Wih', 'Whh', 'bih', 'bhh')}
    del _L0_gnn_all

    def _L0_ffn_setup():
        import jax, jax.numpy as jnp
        import numpy as np
        B, K, D = (256, 16, 128)
        E = 32
        H = int(D * 0.25)
        key = jax.random.key(seed)
        ks = jax.random.split(key, 7)
        d_rs = D ** (-0.5)
        h_rs = H ** (-0.5)
        x = jax.random.normal(ks[0], (B, K, D), dtype=jnp.float32)
        router_w = jax.random.uniform(ks[1], (E, D), jnp.float32, -d_rs, d_rs)
        router_b = jax.random.uniform(ks[2], (E,), jnp.float32, -d_rs, d_rs)
        W1 = jax.random.uniform(ks[3], (E, D, H), jnp.float32, -h_rs, h_rs)
        b1 = jax.random.uniform(ks[4], (E, H), jnp.float32, -h_rs, h_rs)
        W2 = jax.random.uniform(ks[5], (E, H, D), jnp.float32, -d_rs, d_rs)
        b2 = jax.random.uniform(ks[6], (E, D), jnp.float32, -d_rs, d_rs)
        return {'x': x, 'router_w': router_w, 'router_b': router_b, 'W1': W1, 'b1': b1, 'W2': W2, 'b2': b2}
    _L0_ffn_all = _L0_ffn_setup()
    _L0_ffn_in = {k: v for k, v in _L0_ffn_all.items() if k in ('router_w', 'router_b', 'W1', 'b1', 'W2', 'b2')}
    del _L0_ffn_all
    return {'x': x, 'adj': adj, 'L0_gnn_Wg0': _L0_gnn_in['Wg0'], 'L0_gnn_bg0': _L0_gnn_in['bg0'], 'L0_gnn_Wg1': _L0_gnn_in['Wg1'], 'L0_gnn_bg1': _L0_gnn_in['bg1'], 'L0_gnn_Wih': _L0_gnn_in['Wih'], 'L0_gnn_Whh': _L0_gnn_in['Whh'], 'L0_gnn_bih': _L0_gnn_in['bih'], 'L0_gnn_bhh': _L0_gnn_in['bhh'], 'L0_ffn_router_w': _L0_ffn_in['router_w'], 'L0_ffn_router_b': _L0_ffn_in['router_b'], 'L0_ffn_W1': _L0_ffn_in['W1'], 'L0_ffn_b1': _L0_ffn_in['b1'], 'L0_ffn_W2': _L0_ffn_in['W2'], 'L0_ffn_b2': _L0_ffn_in['b2']}

def reference(x, adj, L0_gnn_Wg0, L0_gnn_bg0, L0_gnn_Wg1, L0_gnn_bg1, L0_gnn_Wih, L0_gnn_Whh, L0_gnn_bih, L0_gnn_bhh, L0_ffn_router_w, L0_ffn_router_b, L0_ffn_W1, L0_ffn_b1, L0_ffn_W2, L0_ffn_b2):
    import jax
    import jax.numpy as jnp

    def _L0_gnn_ref(x, adj, Wg0, bg0, Wg1, bg1, Wih, Whh, bih, bhh):
        import jax, jax.numpy as jnp
        import numpy as np
        B, T, D, H = (64, 1024, 128, 128)
        MAX_SKIP = 4

        def _lstm_last(Wih, Whh, bih, bhh, xs):
            N, _, Hd = xs.shape
            bias = bih + bhh

            def step(carry, x_t):
                h, c = carry
                g = x_t @ Wih.T + h @ Whh.T + bias
                i, f, gg, o = jnp.split(g, 4, axis=-1)
                c = jax.nn.sigmoid(f) * c + jax.nn.sigmoid(i) * jnp.tanh(gg)
                h = jax.nn.sigmoid(o) * jnp.tanh(c)
                return ((h, c), None)
            init = (jnp.zeros((N, Hd), xs.dtype), jnp.zeros((N, Hd), xs.dtype))
            (h_last, _), _ = jax.lax.scan(step, init, jnp.swapaxes(xs, 0, 1))
            return h_last
        h = jax.nn.relu(jnp.einsum('ts,bsh->bth', adj, x @ Wg0 + bg0))
        h = jax.nn.relu(jnp.einsum('ts,bsh->bth', adj, h @ Wg1 + bg1))
        Bv, Tv, Hd = h.shape
        for p in range(1, MAX_SKIP + 1):
            nw = Tv // p
            wins = h[:, :nw * p, :].reshape(Bv * nw, p, Hd)
            last = _lstm_last(Wih[p - 1], Whh[p - 1], bih[p - 1], bhh[p - 1], wins)
            idx = jnp.arange(nw) * p + (p - 1)
            h = h.at[:, idx, :].set(last.reshape(Bv, nw, Hd))
        return h

    def _L0_ffn_ref(x, router_w, router_b, W1, b1, W2, b2):
        import jax, jax.numpy as jnp
        import numpy as np
        B, K, D = (256, 16, 128)
        E = 32
        H = int(D * 0.25)
        xf = x.reshape(-1, D)
        logits = xf @ router_w.T + router_b
        idx = jnp.argmax(logits, axis=-1)
        w1t = jnp.take(W1, idx, axis=0)
        h = jnp.einsum('nd,ndh->nh', xf, w1t) + jnp.take(b1, idx, axis=0)
        h = jax.nn.relu(h)
        w2t = jnp.take(W2, idx, axis=0)
        out = jnp.einsum('nh,nhd->nd', h, w2t) + jnp.take(b2, idx, axis=0)
        out = jax.nn.relu(out)
        return out.reshape(x.shape)
    x = x + _L0_gnn_ref(_layernorm(x, axis=-1), adj, L0_gnn_Wg0, L0_gnn_bg0, L0_gnn_Wg1, L0_gnn_bg1, L0_gnn_Wih, L0_gnn_Whh, L0_gnn_bih, L0_gnn_bhh)
    x = x + _L0_ffn_ref(_layernorm(x, axis=-1), L0_ffn_router_w, L0_ffn_router_b, L0_ffn_W1, L0_ffn_b1, L0_ffn_W2, L0_ffn_b2)
    return x

_drawn_inputs = setup_inputs


def setup_inputs(seed=0):
    import zlib

    import numpy as np

    out = dict(_drawn_inputs(seed))
    spreads = {'L0_gnn_bg0': (0.0, 0.8), 'L0_gnn_bg1': (0.0, 0.8)}
    factors = {'adj': 8.0,
     'L0_gnn_Wg0': 8.0,
     'L0_gnn_Wg1': 8.0,
     'L0_gnn_Wih': 5.205,
     'L0_gnn_Whh': 5.102,
     'L0_ffn_b1': 4.087}
    for name, (base, spread) in spreads.items():
        noise = np.random.default_rng([zlib.crc32(name.encode()), seed]).standard_normal(out[name].shape)
        drawn = base * np.exp(spread * noise) if base else spread * noise
        out[name] = jnp.asarray(drawn.astype(out[name].dtype))
    for name, factor in factors.items():
        out[name] = (out[name] * factor).astype(out[name].dtype)
    return out
```

```python
from contextlib import ExitStack

import concourse.bass as bass
from concourse import mybir

F32 = mybir.dt.float32
F32R = mybir.dt.float32r
BF16 = mybir.dt.bfloat16
ALU = mybir.AluOpType
ACT = mybir.ActivationFunctionType
AX = mybir.AxisListType

P = 128
GB = 4
HALF = 512
EPS = 1e-5
UNPICKED = -1e30

I_, F_, G_, O_ = 0, 1, 2, 3


def lstm_steps(max_p):
    steps = [(1, 0, 0), (1, 0, 1)]
    for p in range(2, max_p + 1):
        steps += [(p, s, None) for s in range(p)]
    return steps


def gates_of(s):
    return (I_, G_, O_) if s == 0 else (I_, G_, F_, O_)


STEPS = lstm_steps(4)
NSTEP = len(STEPS)
TILE = {}
for _n, (_p, _s, _c) in enumerate(STEPS):
    for _q in gates_of(_s):
        TILE[_n, _q] = len(TILE)
NTILE = len(TILE)


def tile_before(n, gate):
    for m in range(n - 1, -1, -1):
        if (m, gate) in TILE:
            return 0, TILE[m, gate]
    return 1, max(t for (m, q), t in TILE.items() if q == gate)


FILL = [
    [("mt", 0), ("ln1", 0)],
    [("gy", 0)],
    [("mx", 0), ("gy", 1)],
    [("ml", 0), ("gw", 0)],
    [("mo", 0), ("gw", 1), ("gz", 0)],
    [("mw", 0), ("mw", 1), ("gz", 1), ("mw", 2)],
    [("mw", 3), ("mw", 4), ("ga", 0), ("mw", 5)],
    [("mw", 6), ("mw", 7), ("ga", 1), ("mw", 8)],
    [("mw", 9), ("me", 0), ("mw", 10)],
    [("mw", 11), ("mw", 12)],
    [("mw", 13), ("mw", 14), ("mw", 15), ("me", 1)],
]
GNN_UNIT = {"gy": 0, "gw": 2, "gz": 4, "ga": 6}
NGNN = 8
NW = 16


def moe_units():
    units, n = {}, 0
    for slot in FILL:
        for kind, k in slot:
            if kind in ("mt", "mx"):
                units[kind, 0], units[kind, 1] = n, n + 1
                n += 2
            elif kind in ("ml", "mo", "mw", "me"):
                units[kind, k] = n
                n += 1
    return units


MU = moe_units()
NMOE = len(MU)
assert NMOE % 2 == 0

SETUP = ["adj", "bm0", "wg0", "wg1", "bias"] + [f"ih{p}" for p in range(4)] + \
        [f"hh{p}" for p in range(1, 4)] + ["router", "w1", "w2", "b2"]
SETUP_AT = {name: n + 1 for n, name in enumerate(SETUP)}
SETUP_PE = ["adj", "bm0", "bias"] + [f"ih{p}" for p in range(4)] + [f"hh{p}" for p in range(1, 4)]
SETUP_PE_AT = {name: n + 1 for n, name in enumerate(SETUP_PE)}
SETUP_ACT = ["adj", "wg0", "wg1"] + [f"ih{p}" for p in range(4)] + [f"hh{p}" for p in range(1, 4)] + \
            ["router", "w1", "w2"]
SETUP_ACT_AT = {name: n + 1 for n, name in enumerate(SETUP_ACT)}


def gnn_lstm_moe(nc, x, adj, Wg0, bg0, Wg1, bg1, Wih, Whh, bih, bhh, router_w, router_b, W1, b1, W2, b2, out):
    B, T, D = x.shape
    NG = B // GB
    TOK = GB * T
    KT = T // P
    TILES = TOK // P
    E, _, HE = W1.shape
    EQ = E * HE // P
    EPT = P // HE
    MP = Wih.shape[0]
    assert D == P and KT == 2 and TILES == 8 and EQ == 8 and MP == 4 and TOK == 2 * HALF and E == 32

    ctx = ExitStack()
    with ctx:
        def sb(name, shape, dt=F32):
            return ctx.enter_context(nc.sbuf_tensor(name, shape, dt))

        def sem(name):
            return ctx.enter_context(nc.semaphore(name))

        ident = sb("ident", [P, P])
        ident16 = sb("ident16", [P, P], BF16)
        ones_r = sb("ones_r", [P, P], F32R)
        adjT_hi, adjT_lo = (sb(f"adjT_{v}", [P, KT, T], F32R) for v in ("hi", "lo"))
        wg_hi, wg_lo = (sb(f"wg_{v}", [P, 2, P], F32R) for v in ("hi", "lo"))
        wih_hi, wih_lo = (sb(f"wih_{v}", [P, MP, 4 * P], F32R) for v in ("hi", "lo"))
        whh_hi, whh_lo = (sb(f"whh_{v}", [P, MP - 1, 4 * P], F32R) for v in ("hi", "lo"))
        w1_hi, w1_lo = (sb(f"w1_{v}", [P, E * HE], F32R) for v in ("hi", "lo"))
        w2_hi, w2_lo = (sb(f"w2_{v}", [P, EQ, P], F32R) for v in ("hi", "lo"))
        rT_hi, rT_lo = (sb(f"rT_{v}", [P, E], F32R) for v in ("hi", "lo"))
        wg_raw = sb("wg_raw", [P, 2, P])
        adj_raw = sb("adj_raw", [P, KT, T])
        r_raw = sb("r_raw", [E, P])
        b_raw = sb("b_raw", [4 * MP, 2, P])
        bsum = sb("bsum", [4 * MP, P])
        rb = sb("rb", [P, E])
        bg0col = sb("bg0col", [P, 1])
        bg1row = sb("bg1row", [P, P])
        bm0 = sb("bm0", [P, T])
        gbias = sb("gbias", [P, 4 * MP])
        b1_raw = sb("b1_raw", [3 * E, HE])
        b2_raw = sb("b2_raw", [3 * E, P])
        b1_rest = sb("b1_rest", [3 * E, 2, HE])
        b2_rest = sb("b2_rest", [3 * E, 2, P])
        b1_part = sb("b1_part", [3 * E, 3, HE], BF16)
        b2_part = sb("b2_part", [3 * E, 3, P], BF16)
        b1_sel = sb("b1_sel", [3 * E, EQ, EPT, HE], BF16)
        b2_sel = sb("b2_sel", [3 * E, P], BF16)
        rank = sb("rank", [P, E])
        half_neg = sb("half_neg", [P, TILES])

        pause = sb("pause", [P, 1])

        x_nat = sb("x_nat", [P, TILES, P])
        st1 = sb("st1", [P, TILES, 6])
        mv1 = sb("mv1", [P, TILES, 2])
        ve1 = sb("ve1", [P, TILES])
        rs1 = sb("rs1", [P, TILES])
        xn = sb("xn", [P, TILES, P])
        xn_hi, xn_lo = (sb(f"xn_{v}", [P, TILES, P], F32R) for v in ("hi", "lo"))
        yz_hi, yz_lo = (sb(f"yz_{v}", [P, 2, HALF], F32R) for v in ("hi", "lo"))
        gf = sb("gf", [P, 2, HALF])
        h1_hi, h1_lo = (sb(f"h1_{v}", [P, 2, HALF], F32R) for v in ("hi", "lo"))
        hin_hi, hin_lo = (sb(f"hin_{v}", [P, TOK], F32R) for v in ("hi", "lo"))
        hb_hi, hb_lo = (sb(f"hb_{v}", [P, T, GB], F32R) for v in ("hi", "lo"))
        gact = sb("gact", [P, 2, 4, HALF])
        cell = sb("cell", [P, HALF])
        ig = sb("ig", [P, HALF])
        fc = sb("fc", [P, HALF])
        tc = sb("tc", [P, HALF])
        hf = sb("hf", [P, HALF])
        hs_hi, hs_lo = (sb(f"hs_{v}", [P, HALF], F32R) for v in ("hi", "lo"))
        hfull = sb("hfull", [P, GB, T])
        x_res = sb("x_res", [P, TILES, P])
        x2 = sb("x2", [P, TILES, P])
        st2 = sb("st2", [P, TILES, 6])
        mv2 = sb("mv2", [P, TILES, 2])
        ve2 = sb("ve2", [P, TILES])
        rs2 = sb("rs2", [P, TILES])
        xn2 = sb("xn2", [P, TILES, P])
        xT_hi, xT_lo = (sb(f"xT_{v}", [P, TOK], F32R) for v in ("hi", "lo"))
        lg = sb("lg", [P, TILES, E])
        lmax = sb("lmax", [P, TILES, 1])
        cand = sb("cand", [P, TILES, E])
        best = sb("best", [P, TILES, 1])
        oh3 = sb("oh3", [P, TILES, 3 * E], BF16)
        ohT = sb("ohT", [3 * E, TOK], BF16)
        hm_hi, hm_lo = (sb(f"hm_{v}", [P, 2, HALF], F32R) for v in ("hi", "lo"))
        orel = sb("orel", [P, HALF])
        obuf = sb("obuf", [P, TILES, P])
        wih_raw = gact[:, 0, :, :].rearrange("p q (r c) -> p (q r) c", c=P)
        whh_raw = gact[:, 1, :, :].rearrange("p q (r c) -> p (q r) c", c=P)
        w1_raw = obuf[:, :, :].rearrange("p a b -> p (a b)")
        w2_raw = xn2

        gate_ps = [ctx.enter_context(nc.psum_tensor(f"gate_ps{q}", [P, HALF], F32)) for q in range(4)]
        gnn_ps = ctx.enter_context(nc.psum_tensor("gnn_ps", [P, HALF], F32))
        moe_ps = [ctx.enter_context(nc.psum_tensor(f"moe_ps{q}", [P, HALF], F32)) for q in range(2)]
        acc_ps = ctx.enter_context(nc.psum_tensor("acc_ps", [P, HALF], F32))

        adj_loaded, w_loaded = sem("adj_loaded"), sem("w_loaded")
        xnat_loaded, xres_loaded = sem("xnat_loaded"), sem("xres_loaded")
        stored = [sem(f"stored{h}") for h in range(2)]
        const_made = sem("const_made")
        b1_split = sem("b1_split")
        b1_sel_made = sem("b1_sel_made")
        setup_pe, setup_hi, setup_done = sem("setup_pe"), sem("setup_hi"), sem("setup_done")
        dve_tmp = sem("dve_tmp")
        ln1_stat, ln1_aggr, ln1_var, ln1_rstd = sem("ln1_stat"), sem("ln1_aggr"), sem("ln1_var"), sem("ln1_rstd")
        ln1_read, ln1_hi, xn_ready = sem("ln1_read"), sem("ln1_hi"), sem("xn_ready")
        gnn_ready, gnn_biased, gnn_hi, gnn_drained = sem("gnn_ready"), sem("gnn_biased"), sem("gnn_hi"), sem("gnn_drained")
        gate_ready, gate_done = sem("gate_ready"), sem("gate_done")
        prod_ready, cell_ready, tanh_ready = sem("prod_ready"), sem("cell_ready"), sem("tanh_ready")
        hf_ready, h_hi_ready, h_lo_ready = sem("hf_ready"), sem("h_hi_ready"), sem("h_lo_ready")
        hfull_ready = sem("hfull_ready")
        moe_ready = sem("moe_ready")
        moe_drained = [sem(f"moe_drained{q}") for q in range(2)]
        ln2_stat, ln2_aggr, ln2_var, ln2_rstd, xn2_ready = (
            sem("ln2_stat"), sem("ln2_aggr"), sem("ln2_var"), sem("ln2_rstd"), sem("xn2_ready"))
        xT_hi_ready, oh_step, hm_hi_ready, w2_used, acc_ready, orel_ready = (
            sem("xT_hi_ready"), sem("oh_step"), sem("hm_hi_ready"), sem("w2_used"), sem("acc_ready"), sem("orel_ready"))

        x_v = x.rearrange("(n b) (k s) d -> n s (b k) d", b=GB, s=P)
        out_v = out.rearrange("(n b) (k s) d -> n s (b k) d", b=GB, s=P)

        def columns(n):
            p, s, chunk = STEPS[n]
            return HALF if p == 1 else (T // p) * GB

        def tokens(hi_or_lo, n, last=False):
            p, s, chunk = STEPS[n]
            if p == 1:
                v = hi_or_lo if last is False else hi_or_lo[:, :, :].rearrange("p t b -> p (t b)")
                return v[:, chunk * HALF:(chunk + 1) * HALF]
            a = p - 1 if last else s
            return hi_or_lo[:, a:a + p * (T // p - 1) + 1:p, :]

        def as_tokens(flat, n):
            return flat if STEPS[n][0] == 1 else flat.rearrange("p (t b) -> p t b", b=GB)

        def is_last(n):
            p, s, _ = STEPS[n]
            return s == p - 1

        def wait(eng, s, g, per_group, value):
            if isinstance(g, int):
                if per_group * g + value > 0:
                    eng.wait_ge(s, per_group * g + value)
            else:
                eng.wait_ge(s, g * per_group + value)

        def moe_free(eng, g, unit):
            wait(eng, moe_drained[unit % 2], g, NMOE // 2, unit // 2)

        def moe_is_drained(eng, g, unit):
            wait(eng, moe_drained[unit % 2], g, NMOE // 2, unit // 2 + 1)

        def x2_is_taken(eng, g):
            if not (isinstance(g, int) and g < 0):
                moe_is_drained(eng, g, MU["mt", 0])
                moe_is_drained(eng, g, MU["mt", 1])

        block = ctx.enter_context(nc.Block())

        def iterations(eng, body):
            body(0, 1, None)
            body(1, 2, 0)
            with eng.Fori(2, NG - 1) as i:
                body(i, i + 1, i - 1)
            body(NG - 1, None, NG - 2)

        @block.sync
        def _(sp):
            sp.dma_start(adj_raw[:, :, :], adj.rearrange("(k t) s -> t k s", t=P)).then_inc(adj_loaded, 16)
            sp.dma_start(x_nat[:, :, :], x_v[0]).then_inc(xnat_loaded, 16)
            loads = [
                (wg_raw[:, 0, :], Wg0), (wg_raw[:, 1, :], Wg1),
                (bg0col[:, :], bg0.rearrange("(h a) -> h a", a=1)),
                (bg1row[:, :], bg1.partition_broadcast(P)),
                (b_raw[:, 0, :], bih.rearrange("p (q h) -> (p q) h", h=P)),
                (b_raw[:, 1, :], bhh.rearrange("p (q h) -> (p q) h", h=P)),
                (wih_raw, Wih.rearrange("p (q a) h -> a (p q) h", a=P)),
                (whh_raw, Whh.rearrange("p (q a) h -> a (p q) h", a=P)),
                (r_raw[:, :], router_w), (rb[:, :], router_b.partition_broadcast(P)),
                (w1_raw.rearrange("p (e h) -> p e h", h=HE), W1.rearrange("e d h -> d e h")),
                (w2_raw[:, :, :], W2.rearrange("(q e) h d -> (e h) q d", e=EPT)),
            ]
            loads += [(b1_raw[E * r:E * r + E, :], b1) for r in range(3)]
            loads += [(b2_raw[E * r:E * r + E, :], b2) for r in range(3)]
            for dst, src in loads:
                sp.dma_start(dst, src).then_inc(w_loaded, 16)
            assert len(loads) == N_LOADS

            def body(i, g_gnn, g_moe):
                if g_gnn is not None:
                    wait(sp, ln1_read, g_gnn, 1, 0)
                    sp.dma_start(x_nat[:, :, :], x_v[g_gnn]).then_inc(xnat_loaded, 16)
                if g_moe is not None:
                    x2_is_taken(sp, g_moe - 1)
                    sp.dma_start(x_res[:, :, :], x_v[g_moe]).then_inc(xres_loaded, 16)

            iterations(sp, body)
            x2_is_taken(sp, NG - 2)
            sp.dma_start(x_res[:, :, :], x_v[NG - 1]).then_inc(xres_loaded, 16)

        @block.gpsimd
        def _(pool):
            nc.gpsimd.memset(ident[:, :], 0.0).then_inc(const_made, 1)
            nc.gpsimd.memset(ident16[:, :], 0.0).then_inc(const_made, 1)
            nc.gpsimd.memset(ones_r[:, :].bitcast(F32), 1.0).then_inc(const_made, 1)
            nc.gpsimd.memset(half_neg[:, :], -0.5).then_inc(const_made, 1)
            nc.gpsimd.iota(rank[:, :], pattern=[[-1, E]], base=E, channel_multiplier=0,
                           allow_small_or_imprecise_dtypes=True).then_inc(const_made, 1)
            pool.wait_ge(const_made, 5)
            for m in (ident, ident16):
                nc.gpsimd.affine_select(out=m[:, :], in_=m[:, :], compare_op=ALU.not_equal, fill=1.0, base=0,
                                        pattern=[[-1, P]], channel_multiplier=1).then_inc(const_made, 1)

            def power(g, var, rs, ready, done):
                wait(pool, ready, g, 1, 1)
                nc.gpsimd.tensor_tensor(rs[:, :], var[:, :], half_neg[:, :], ALU.pow).then_inc(done, 1)

            def store(g, half):
                moe_is_drained(pool, g, MU["me", half])
                q = TILES // 2
                pool.dma_start(out_v[g][:, half * q:half * q + q, :], obuf[:, half * q:half * q + q, :])\
                    .then_inc(stored[half], 16)

            def whole_h(g):
                wait(pool, h_lo_ready, g, NSTEP, NSTEP)
                if not (isinstance(g, int) and g == 0):
                    wait(pool, moe_ready, g, NMOE, MU["mt", 1] + 1 - NMOE)
                o = hfull[:, :, :].rearrange("p b t -> p t b")
                nc.gpsimd.tensor_tensor(o, hb_hi[:, :, :].bitcast(F32), hb_lo[:, :, :].bitcast(F32), ALU.add)\
                    .then_inc(hfull_ready, 1)

            power(0, ve1, rs1, ln1_var, ln1_rstd)
            pool.wait_ge(b1_split, 1)
            pool.wait_ge(ln1_rstd, 1)
            for r in range(3):
                if r > 0:
                    pool.wait_ge(b1_sel_made, r)
                src = b1_part[E * r:E * r + E, r, :].unsqueeze(1).to_broadcast([E, E, HE])
                nc.gpsimd.affine_select(
                    out=b1_sel[E * r:E * r + E, :, :, :].rearrange("p q e h -> p (q e) h"), in_=src,
                    compare_op=ALU.is_equal, fill=UNPICKED if r == 0 else 0.0, base=0,
                    pattern=[[-1, E], [0, HE]], channel_multiplier=1).then_inc(b1_sel_made, 1)

            pool.wait_ge(b1_sel_made, 3)

            def body(i, g_gnn, g_moe):
                if g_moe is not None:
                    power(g_moe, ve2, rs2, ln2_var, ln2_rstd)
                if g_gnn is not None:
                    power(g_gnn, ve1, rs1, ln1_var, ln1_rstd)
                if g_moe is not None:
                    store(g_moe, 0)
                whole_h(i)
                if g_moe is not None:
                    store(g_moe, 1)

            iterations(pool, body)
            power(NG - 1, ve2, rs2, ln2_var, ln2_rstd)
            store(NG - 1, 0)
            store(NG - 1, 1)
            for half in range(2):
                pool.wait_ge(stored[half], 16 * NG)

        @block.tensor
        def _(pe):
            def three(o, w_hi, w_lo, r_hi, r_lo, start, stop):
                nc.tensor.matmul(o, w_hi, r_hi, start=start, stop=False)
                nc.tensor.matmul(o, w_lo, r_hi, start=False, stop=False)
                return nc.tensor.matmul(o, w_hi, r_lo, start=False, stop=stop)

            pe.wait_ge(const_made, 7)
            pe.wait_ge(adj_loaded, 16)
            for k in range(KT):
                for t in range(KT):
                    mm = nc.tensor.transpose(gnn_ps[:, k * T + t * P:k * T + t * P + P],
                                             adj_raw[:, t, k * P:k * P + P], ident[:, :])
            mm.then_inc(setup_pe, 1)
            pe.wait_ge(setup_done, SETUP_AT["adj"])
            for k in range(KT):
                nc.tensor.matmul(moe_ps[0][:, 0:T], ones_r[:, :], adjT_hi[:, k, :], start=(k == 0), stop=False)
                mm = nc.tensor.matmul(moe_ps[0][:, 0:T], ones_r[:, :], adjT_lo[:, k, :], start=False, stop=(k == KT - 1))
            mm.then_inc(setup_pe, 1)
            pe.wait_ge(w_loaded, 16 * N_LOADS)
            pe.wait_ge(dve_tmp, 1)
            nc.tensor.transpose(moe_ps[1][:, 0:E], r_raw[:, :], ident[0:E, 0:E])
            nc.tensor.transpose(moe_ps[1][:, E:E + 4 * MP], bsum[:, :], ident[0:4 * MP, 0:4 * MP])\
                .then_inc(setup_pe, 1)
            for n, name in enumerate(SETUP_PE[3:]):
                raw, p = (wih_raw, int(name[2])) if name[0] == "i" else (whh_raw, int(name[2]))
                if n >= 4:
                    pe.wait_ge(setup_done, SETUP_AT[SETUP_PE[3 + n - 4]])
                for q in range(4):
                    mm = nc.tensor.transpose(gate_ps[n % 4][:, q * P:q * P + P], raw[:, 4 * p + q, :], ident[:, :])
                mm.then_inc(setup_pe, 1)

            def gnn(kind, g, u):
                unit = GNN_UNIT[kind] + u
                wait(pe, gnn_drained, g, NGNN, unit)
                if kind == "gy":
                    wait(pe, xn_ready, g, 1, 1)
                    for bb in range(2):
                        o = gnn_ps[:, bb * T:bb * T + T]
                        for k in range(KT):
                            j = (2 * u + bb) * KT + k
                            mm = three(o, xn_hi[:, j, :], xn_lo[:, j, :], adjT_hi[:, k, :], adjT_lo[:, k, :],
                                       k == 0, k == KT - 1)
                elif kind == "gw":
                    mm = three(gnn_ps[:, :], wg_hi[:, 0, :], wg_lo[:, 0, :], yz_hi[:, u, :], yz_lo[:, u, :], True, True)
                elif kind == "gz":
                    for j in range(2 * KT):
                        c = slice(j * P, j * P + P)
                        mm = three(gnn_ps[:, c], h1_hi[:, u, c], h1_lo[:, u, c], wg_hi[:, 1, :], wg_lo[:, 1, :],
                                   True, True)
                else:
                    for bb in range(2):
                        o = gnn_ps[:, bb * T:bb * T + T]
                        for k in range(KT):
                            c = slice((bb * KT + k) * P, (bb * KT + k) * P + P)
                            mm = three(o, yz_hi[:, u, c], yz_lo[:, u, c], adjT_hi[:, k, :], adjT_lo[:, k, :],
                                       k == 0, k == KT - 1)
                mm.then_inc(gnn_ready, 1)

            def gates_x(g, n):
                p, s, _ = STEPS[n]
                N = columns(n)
                if p == 1:
                    wait(pe, gnn_drained, g, NGNN, NGNN)
                    r_hi, r_lo = tokens(hin_hi, n), tokens(hin_lo, n)
                else:
                    r_hi, r_lo = tokens(hb_hi, n), tokens(hb_lo, n)
                    if s == 0:
                        wait(pe, h_lo_ready, g, NSTEP, n)
                for q in gates_of(s):
                    back, t = tile_before(n, q)
                    wait(pe, gate_done, g, NTILE, t + 1 - back * NTILE)
                    c = slice(q * P, q * P + P)
                    mm = three(as_tokens(gate_ps[q][:, 0:N], n), wih_hi[:, p - 1, c], wih_lo[:, p - 1, c],
                               r_hi, r_lo, True, s == 0)
                    if s == 0:
                        mm.then_inc(gate_ready, 1)

            def gates_h(g, n):
                p, s, _ = STEPS[n]
                N = columns(n)
                wait(pe, h_hi_ready, g, NSTEP, n)
                for q in gates_of(s):
                    c = slice(q * P, q * P + P)
                    nc.tensor.matmul(gate_ps[q][:, 0:N], whh_hi[:, p - 2, c], hs_hi[:, 0:N], start=False, stop=False)
                    nc.tensor.matmul(gate_ps[q][:, 0:N], whh_lo[:, p - 2, c], hs_hi[:, 0:N], start=False, stop=False)
                wait(pe, h_lo_ready, g, NSTEP, n)
                for q in gates_of(s):
                    nc.tensor.matmul(gate_ps[q][:, 0:N], whh_hi[:, p - 2, q * P:q * P + P], hs_lo[:, 0:N],
                                     start=False, stop=True).then_inc(gate_ready, 1)

            def second_product(g, n):
                half, q = divmod(n, EQ)
                if q == 0:
                    wait(pe, orel_ready, g, 2, half)
                moe_is_drained(pe, g, MU["mw", n])
                o = acc_ps[:, :]
                mm = three(o, w2_hi[:, q, :], w2_lo[:, q, :], hm_hi[:, n % 2, :], hm_lo[:, n % 2, :], q == 0, False)
                mm.then_inc(w2_used, 1)
                if q == EQ - 1:
                    nc.tensor.matmul(o, b2_sel[:, :], ohT[:, half * HALF:half * HALF + HALF], start=False, stop=True)\
                        .then_inc(acc_ready, 1)

            def moe(kind, g, k):
                if kind == "mt":
                    wait(pe, hfull_ready, g, 1, 1)
                    for u in range(2):
                        unit = MU["mt", u]
                        moe_free(pe, g, unit)
                        for j in range(4):
                            col = (4 * u + j) * P
                            mm = nc.tensor.transpose(moe_ps[unit % 2][:, j * P:j * P + P],
                                                     hfull[:, :, :].rearrange("p b t -> p (b t)")[:, col:col + P],
                                                     ident[:, :])
                        mm.then_inc(moe_ready, 1)
                elif kind == "mx":
                    for u in range(2):
                        unit = MU["mx", u]
                        moe_free(pe, g, unit)
                        wait(pe, xn2_ready, g, 2, u + 1)
                        for j in range(4):
                            mm = nc.tensor.transpose(moe_ps[unit % 2][:, j * P:j * P + P], xn2[:, 4 * u + j, :],
                                                     ident[:, :])
                        mm.then_inc(moe_ready, 1)
                elif kind == "ml":
                    unit = MU["ml", 0]
                    moe_free(pe, g, unit)
                    moe_is_drained(pe, g, MU["mx", 0])
                    moe_is_drained(pe, g, MU["mx", 1])
                    for j in range(TILES):
                        c = slice(j * P, j * P + P)
                        mm = three(moe_ps[unit % 2][:, j * E:j * E + E], xT_hi[:, c], xT_lo[:, c], rT_hi[:, :], rT_lo[:, :],
                                   True, True)
                    mm.then_inc(moe_ready, 1)
                elif kind == "mo":
                    unit = MU["mo", 0]
                    moe_free(pe, g, unit)
                    wait(pe, oh_step, g, 7, 7)
                    o = moe_ps[unit % 2][:, :].bitcast(BF16)
                    for j in range(TILES):
                        mm = nc.tensor.transpose(o[0:3 * E, j * P:j * P + P], oh3[:, j, :], ident16[:, :])
                    mm.then_inc(moe_ready, 1)
                elif kind == "mw":
                    unit = MU["mw", k]
                    half, q = divmod(k, EQ)
                    moe_free(pe, g, unit)
                    if k == 0:
                        moe_is_drained(pe, g, MU["mo", 0])
                    o = moe_ps[unit % 2][:, :]
                    c = slice(half * HALF, half * HALF + HALF)
                    nc.tensor.matmul(o, b1_sel[:, q, :, :].rearrange("p e h -> p (e h)"), ohT[:, c],
                                     start=True, stop=False)
                    three(o, w1_hi[:, q * P:q * P + P], w1_lo[:, q * P:q * P + P], xT_hi[:, c], xT_lo[:, c],
                          False, True).then_inc(moe_ready, 1)
                    if k > 0:
                        second_product(g, k - 1)
                else:
                    unit = MU["me", k]
                    if k == 1:
                        second_product(g, NW - 1)
                    moe_free(pe, g, unit)
                    wait(pe, orel_ready, g, 2, k + 1)
                    for j in range(4):
                        mm = nc.tensor.transpose(moe_ps[unit % 2][:, j * P:j * P + P], orel[:, j * P:j * P + P],
                                                 ident[:, :])
                    mm.then_inc(moe_ready, 1)

            def fill(slot, g_gnn, g_moe):
                for kind, k in FILL[slot]:
                    if kind in GNN_UNIT and g_gnn is not None:
                        gnn(kind, g_gnn, k)
                    elif kind[0] == "m" and g_moe is not None:
                        moe(kind, g_moe, k)

            pe.wait_ge(setup_done, SETUP_AT["wg1"])
            for kind in ("gy", "gw", "gz", "ga"):
                for u in range(2):
                    gnn(kind, 0, u)
            pe.wait_ge(setup_done, SETUP_AT["b2"])
            pe.wait_ge(b1_sel_made, 3)

            def body(i, g_gnn, g_moe):
                for n in range(NSTEP):
                    p, s, _ = STEPS[n]
                    if s == 0:
                        gates_x(i, n)
                    else:
                        gates_h(i, n)
                    if n + 1 < NSTEP and STEPS[n + 1][1] > 0:
                        gates_x(i, n + 1)
                    fill(n, g_gnn, g_moe)

            iterations(pe, body)
            for slot in range(NSTEP):
                fill(slot, None, NG - 1)

        @block.scalar
        def _(act):
            def hi_of(dst, src):
                return nc.scalar.copy(dst, src)

            act.wait_ge(setup_pe, SETUP_PE_AT["adj"])
            hi_of(adjT_hi[:, :, :].rearrange("p k t -> p (k t)"), gnn_ps[:, :]).then_inc(setup_hi, 1)
            act.wait_ge(w_loaded, 16 * N_LOADS)
            for n in range(2):
                hi_of(wg_hi[:, n, :], wg_raw[:, n, :]).then_inc(setup_hi, 1)
            for n, name in enumerate(SETUP_PE[3:]):
                act.wait_ge(setup_pe, SETUP_PE_AT[name])
                dst = wih_hi[:, n, :] if n < 4 else whh_hi[:, n - 4, :]
                hi_of(dst, gate_ps[n % 4][:, :]).then_inc(setup_hi, 1)
            act.wait_ge(setup_pe, SETUP_PE_AT["bias"])
            hi_of(rT_hi[:, :], moe_ps[1][:, 0:E]).then_inc(setup_hi, 1)
            hi_of(w1_hi[:, :], w1_raw).then_inc(setup_hi, 1)
            hi_of(w2_hi[:, :, :], w2_raw[:, :, :]).then_inc(setup_hi, 1)

            def ln1(g):
                wait(act, ln1_read, g, 1, 1)
                hi_of(xn_hi[:, :, :], xn[:, :, :]).then_inc(ln1_hi, 1)

            def gnn(kind, g, u):
                unit = GNN_UNIT[kind] + u
                if kind in ("gw", "gz"):
                    wait(act, gnn_biased, g, 4, unit - 1)
                    if kind == "gw":
                        a = nc.scalar.activation(h1_hi[:, u, :], gf[:, u, :], ACT.Relu)
                    else:
                        a = hi_of(yz_hi[:, u, :], gf[:, u, :])
                else:
                    wait(act, gnn_ready, g, NGNN, unit + 1)
                    if kind == "gy":
                        a = hi_of(yz_hi[:, u, :], gnn_ps[:, :])
                    else:
                        o = hin_hi[:, :].rearrange("p (t b) -> p b t", b=GB)[:, 2 * u:2 * u + 2, :]
                        a = nc.scalar.activation(o, gnn_ps[:, :].rearrange("p (b t) -> p b t", b=2), ACT.Relu)
                a.then_inc(gnn_hi, 1)

            def lstm(g, n):
                p, s, _ = STEPS[n]
                N = columns(n)
                if n == 0:
                    wait(act, h_hi_ready, g, NSTEP, 0)
                for q in gates_of(s):
                    wait(act, gate_ready, g, NTILE, TILE[n, q] + 1)
                    nc.scalar.activation(gact[:, n % 2, q, 0:N], gate_ps[q][:, 0:N], ACT.Tanh if q == G_ else ACT.Sigmoid,
                                         bias=gbias[:, 4 * (p - 1) + q:4 * (p - 1) + q + 1]).then_inc(gate_done, 1)
                wait(act, cell_ready, g, NSTEP, n + 1)
                nc.scalar.activation(tc[:, 0:N], cell[:, 0:N], ACT.Tanh).then_inc(tanh_ready, 1)

            def moe(kind, g, k):
                if kind == "mx":
                    for u in range(2):
                        unit = MU["mx", u]
                        wait(act, moe_ready, g, NMOE, unit + 1)
                        hi_of(xT_hi[:, u * HALF:u * HALF + HALF], moe_ps[unit % 2][:, :]).then_inc(xT_hi_ready, 1)
                elif kind == "mo":
                    unit = MU["mo", 0]
                    wait(act, moe_ready, g, NMOE, unit + 1)
                    nc.scalar.copy(ohT[:, :], moe_ps[unit % 2][:, :].bitcast(BF16)[0:3 * E, :])\
                        .then_inc(moe_drained[unit % 2], 1)
                elif kind == "mw":
                    unit = MU["mw", k]
                    wait(act, w2_used, g, NW, k - 1)
                    wait(act, moe_ready, g, NMOE, unit + 1)
                    nc.scalar.activation(hm_hi[:, k % 2, :], moe_ps[unit % 2][:, :], ACT.Relu).then_inc(hm_hi_ready, 1)
                elif kind == "me":
                    wait(act, acc_ready, g, 2, k + 1)
                    nc.scalar.activation(orel[:, :], acc_ps[:, :], ACT.Relu).then_inc(orel_ready, 1)

            def fill(slot, g_gnn, g_moe):
                for kind, k in FILL[slot]:
                    if kind == "ln1" and g_gnn is not None:
                        ln1(g_gnn)
                    elif kind in GNN_UNIT and g_gnn is not None:
                        gnn(kind, g_gnn, k)
                    elif kind[0] == "m" and g_moe is not None:
                        moe(kind, g_moe, k)

            ln1(0)
            for kind in ("gy", "gw", "gz", "ga"):
                for u in range(2):
                    gnn(kind, 0, u)
            act.wait_ge(setup_done, SETUP_AT["bias"])

            def body(i, g_gnn, g_moe):
                for n in range(NSTEP):
                    lstm(i, n)
                    fill(n, g_gnn, g_moe)

            iterations(act, body)
            for slot in range(NSTEP):
                fill(slot, None, NG - 1)

        @block.vector
        def _(dve):
            links = [0]

            def link(ins):
                links[0] += 1
                ins.then_inc(dve_tmp, 1)
                dve.wait_ge(dve_tmp, links[0])

            def lo_of(dst, src, hi, op0=ALU.max, scalar=None):
                if scalar is None:
                    return nc.vector.tensor_tensor(dst, src, hi.bitcast(F32), ALU.subtract)
                return nc.vector.scalar_tensor_tensor(out=dst, in0=src, scalar=scalar, in1=hi.bitcast(F32), op0=op0,
                                                      op1=ALU.subtract)

            def normalise(g, src, st, mv, ve, rs, dst, stat, aggr, var, rstd, sems):
                for j in range(TILES):
                    a = nc.vector.bn_stats(st[:, j, :], src[:, j, :])
                a.then_inc(stat, 1)
                wait(dve, stat, g, 1, 1)
                nc.vector.memset(pause[:, :], 0.0)
                for j in range(TILES):
                    a = nc.vector.bn_aggr(mv[:, j, :], st[:, j, :])
                a.then_inc(aggr, 1)
                wait(dve, aggr, g, 1, 1)
                nc.vector.tensor_scalar(ve[:, :], mv[:, :, 1], EPS, None, ALU.add).then_inc(var, 1)
                wait(dve, rstd, g, 1, 1)
                for j in range(TILES):
                    a = nc.vector.tensor_scalar(dst[:, j, :], src[:, j, :], mv[:, j, 0:1], rs[:, j:j + 1],
                                                ALU.subtract, ALU.mult)
                    if j in sems:
                        a.then_inc(sems[j], 1)

            def ln1(g):
                wait(dve, xnat_loaded, g, 16, 16)
                normalise(g, x_nat, st1, mv1, ve1, rs1, xn, ln1_stat, ln1_aggr, ln1_var, ln1_rstd, {TILES - 1: ln1_read})
                wait(dve, ln1_hi, g, 1, 1)
                lo_of(xn_lo[:, :, :], xn[:, :, :], xn_hi[:, :, :]).then_inc(xn_ready, 1)

            def gnn(kind, g, u):
                unit = GNN_UNIT[kind] + u
                if kind in ("gw", "gz"):
                    wait(dve, gnn_ready, g, NGNN, unit + 1)
                    if kind == "gw":
                        bias, shape = bm0[:, :], [P, 2, T]
                    else:
                        bias, shape = bg1row[:, :], [P, 2 * KT, P]
                    view = lambda v: v.rearrange("p (a b) -> p a b", a=shape[1])
                    nc.vector.tensor_tensor(view(gf[:, u, :]), view(gnn_ps[:, :]), bias.unsqueeze(1).to_broadcast(shape),
                                            ALU.add).then_inc(gnn_biased, 1)
                    wait(dve, gnn_hi, g, NGNN, unit + 1)
                    if kind == "gw":
                        a = lo_of(h1_lo[:, u, :], gf[:, u, :], h1_hi[:, u, :], scalar=0.0)
                    else:
                        a = lo_of(yz_lo[:, u, :], gf[:, u, :], yz_hi[:, u, :])
                else:
                    wait(dve, gnn_hi, g, NGNN, unit + 1)
                    if kind == "gy":
                        a = lo_of(yz_lo[:, u, :], gnn_ps[:, :], yz_hi[:, u, :])
                    else:
                        tb = lambda v: v[:, :].rearrange("p (t b) -> p b t", b=GB)[:, 2 * u:2 * u + 2, :]
                        a = lo_of(tb(hin_lo), gnn_ps[:, :].rearrange("p (b t) -> p b t", b=2), tb(hin_hi), scalar=0.0)
                a.then_inc(gnn_drained, 1)

            def lstm(g, n):
                p, s, _ = STEPS[n]
                N = columns(n)
                gate = lambda q: gact[:, n % 2, q, 0:N]
                done = lambda q: wait(dve, gate_done, g, NTILE, TILE[n, q] + 1)
                done(G_)
                if s == 0:
                    nc.vector.tensor_tensor(cell[:, 0:N], gate(I_), gate(G_), ALU.mult).then_inc(cell_ready, 1)
                else:
                    nc.vector.tensor_tensor(ig[:, 0:N], gate(I_), gate(G_), ALU.mult).then_inc(prod_ready, 1)
                    done(F_)
                    nc.vector.tensor_tensor(fc[:, 0:N], gate(F_), cell[:, 0:N], ALU.mult).then_inc(prod_ready, 1)
                    later = [m for m in range(NSTEP) if STEPS[m][1] > 0]
                    wait(dve, prod_ready, g, 2 * len(later), 2 * later.index(n) + 2)
                    nc.vector.tensor_tensor(cell[:, 0:N], ig[:, 0:N], fc[:, 0:N], ALU.add).then_inc(cell_ready, 1)
                done(O_)
                wait(dve, tanh_ready, g, NSTEP, n + 1)
                if n == 0:
                    wait(dve, hfull_ready, g, 1, 0)
                nc.vector.tensor_tensor(hf[:, 0:N], gate(O_), tc[:, 0:N], ALU.mult).then_inc(hf_ready, 1)
                wait(dve, hf_ready, g, NSTEP, n + 1)
                if is_last(n):
                    hi, lo = tokens(hb_hi, n, last=True), tokens(hb_lo, n, last=True)
                    src = as_tokens(hf[:, 0:N], n)
                else:
                    hi, lo, src = hs_hi[:, 0:N], hs_lo[:, 0:N], hf[:, 0:N]
                nc.vector.tensor_copy(hi, src).then_inc(h_hi_ready, 1)
                wait(dve, h_hi_ready, g, NSTEP, n + 1)
                lo_of(lo, src, hi).then_inc(h_lo_ready, 1)

            def moe(kind, g, k):
                if kind == "mt":
                    wait(dve, xres_loaded, g, 16, 16)
                    for u in range(2):
                        unit = MU["mt", u]
                        wait(dve, moe_ready, g, NMOE, unit + 1)
                        nc.vector.tensor_tensor(x2[:, 4 * u:4 * u + 4, :],
                                                moe_ps[unit % 2][:, :].rearrange("p (a b) -> p a b", b=P),
                                                x_res[:, 4 * u:4 * u + 4, :], ALU.add)\
                            .then_inc(moe_drained[unit % 2], 1)
                    x2_is_taken(dve, g)
                    normalise(g, x2, st2, mv2, ve2, rs2, xn2, ln2_stat, ln2_aggr, ln2_var, ln2_rstd,
                              {3: xn2_ready, 7: xn2_ready})
                elif kind == "mx":
                    for u in range(2):
                        unit = MU["mx", u]
                        c = slice(u * HALF, u * HALF + HALF)
                        wait(dve, xT_hi_ready, g, 2, u + 1)
                        lo_of(xT_lo[:, c], moe_ps[unit % 2][:, :], xT_hi[:, c]).then_inc(moe_drained[unit % 2], 1)
                elif kind == "ml":
                    unit = MU["ml", 0]
                    wait(dve, moe_ready, g, NMOE, unit + 1)
                    full = [P, TILES, E]
                    nc.vector.tensor_tensor(lg[:, :, :], moe_ps[unit % 2][:, 0:TILES * E].rearrange("p (a b) -> p a b", b=E),
                                            rb[:, :].unsqueeze(1).to_broadcast(full), ALU.add)\
                        .then_inc(moe_drained[unit % 2], 1)
                    moe_is_drained(dve, g, unit)
                    nc.vector.tensor_reduce(lmax[:, :, 0], lg[:, :, :], AX.X, ALU.max).then_inc(oh_step, 1)
                    wait(dve, oh_step, g, 7, 1)
                    nc.vector.tensor_tensor(cand[:, :, :], lg[:, :, :], lmax[:, :, :].to_broadcast(full), ALU.is_ge)\
                        .then_inc(oh_step, 1)
                    wait(dve, oh_step, g, 7, 2)
                    nc.vector.tensor_tensor(cand[:, :, :], cand[:, :, :], rank[:, :].unsqueeze(1).to_broadcast(full), ALU.mult)\
                        .then_inc(oh_step, 1)
                    wait(dve, oh_step, g, 7, 3)
                    nc.vector.tensor_reduce(best[:, :, 0], cand[:, :, :], AX.X, ALU.max).then_inc(oh_step, 1)
                    wait(dve, oh_step, g, 7, 4)
                    for r in range(3):
                        nc.vector.tensor_tensor(oh3[:, :, r * E:r * E + E], cand[:, :, :], best[:, :, :].to_broadcast(full),
                                                ALU.is_equal).then_inc(oh_step, 1)
                elif kind == "mw":
                    unit = MU["mw", k]
                    wait(dve, hm_hi_ready, g, NW, k + 1)
                    lo_of(hm_lo[:, k % 2, :], moe_ps[unit % 2][:, :], hm_hi[:, k % 2, :], scalar=0.0)\
                        .then_inc(moe_drained[unit % 2], 1)
                elif kind == "me":
                    unit = MU["me", k]
                    wait(dve, moe_ready, g, NMOE, unit + 1)
                    wait(dve, stored[k], g, 16, 0)
                    nc.vector.tensor_tensor(obuf[:, 4 * k:4 * k + 4, :],
                                            moe_ps[unit % 2][:, :].rearrange("p (a b) -> p a b", b=P),
                                            x2[:, 4 * k:4 * k + 4, :], ALU.add).then_inc(moe_drained[unit % 2], 1)

            def fill(slot, g_gnn, g_moe):
                for kind, k in FILL[slot]:
                    if kind == "ln1" and g_gnn is not None:
                        ln1(g_gnn)
                    elif kind in GNN_UNIT and g_gnn is not None:
                        gnn(kind, g_gnn, k)
                    elif kind[0] == "m" and g_moe is not None:
                        moe(kind, g_moe, k)

            dve.wait_ge(setup_hi, SETUP_ACT_AT["adj"])
            lo_of(adjT_lo[:, :, :].rearrange("p k t -> p (k t)"), gnn_ps[:, :],
                  adjT_hi[:, :, :].rearrange("p k t -> p (k t)")).then_inc(setup_done, 1)
            dve.wait_ge(w_loaded, 16 * N_LOADS)
            link(nc.vector.tensor_tensor(bsum[:, :], b_raw[:, 0, :], b_raw[:, 1, :], ALU.add))
            dve.wait_ge(setup_pe, SETUP_PE_AT["bm0"])
            nc.vector.tensor_scalar(bm0[:, :], moe_ps[0][:, 0:T], bg0col[:, 0:1], None, ALU.mult).then_inc(setup_done, 1)
            for n in range(2):
                dve.wait_ge(setup_hi, SETUP_ACT_AT[f"wg{n}"])
                lo_of(wg_lo[:, n, :], wg_raw[:, n, :], wg_hi[:, n, :]).then_inc(setup_done, 1)
            dve.wait_ge(setup_pe, SETUP_PE_AT["bias"])
            nc.vector.tensor_copy(gbias[:, :], moe_ps[1][:, E:E + 4 * MP]).then_inc(setup_done, 1)
            for n, name in enumerate(SETUP_PE[3:]):
                dve.wait_ge(setup_hi, SETUP_ACT_AT[name])
                hi, lo = (wih_hi[:, n, :], wih_lo[:, n, :]) if n < 4 else (whh_hi[:, n - 4, :], whh_lo[:, n - 4, :])
                lo_of(lo, gate_ps[n % 4][:, :], hi).then_inc(setup_done, 1)
            dve.wait_ge(setup_hi, SETUP_ACT_AT["router"])
            lo_of(rT_lo[:, :], moe_ps[1][:, 0:E], rT_hi[:, :]).then_inc(setup_done, 1)
            dve.wait_ge(setup_hi, SETUP_ACT_AT["w1"])
            lo_of(w1_lo[:, :], w1_raw, w1_hi[:, :]).then_inc(setup_done, 1)
            dve.wait_ge(setup_hi, SETUP_ACT_AT["w2"])
            lo_of(w2_lo[:, :, :], w2_raw[:, :, :], w2_hi[:, :, :]).then_inc(setup_done, 1)
            for raw, rest, part in ((b1_raw, b1_rest, b1_part), (b2_raw, b2_rest, b2_part)):
                src = raw[:, :]
                for r in range(3):
                    link(nc.vector.tensor_copy(part[:, r, :], src))
                    if r < 2:
                        link(nc.vector.tensor_tensor(rest[:, r, :], src, part[:, r, :], ALU.subtract))
                        src = rest[:, r, :]
                if raw is b1_raw:
                    nc.vector.engine_nop().then_inc(b1_split, 1)
            for r in range(3):
                a = nc.vector.tensor_copy(b2_sel[E * r:E * r + E, :], b2_part[E * r:E * r + E, r, :])
            a.then_inc(setup_done, 1)

            ln1(0)
            for kind in ("gy", "gw", "gz", "ga"):
                for u in range(2):
                    gnn(kind, 0, u)

            def body(i, g_gnn, g_moe):
                for n in range(NSTEP):
                    lstm(i, n)
                    fill(n, g_gnn, g_moe)

            iterations(dve, body)
            for slot in range(NSTEP):
                fill(slot, None, NG - 1)


N_LOADS = 18

_INS = ["x", "adj", "L0_gnn_Wg0", "L0_gnn_bg0", "L0_gnn_Wg1", "L0_gnn_bg1", "L0_gnn_Wih", "L0_gnn_Whh", "L0_gnn_bih",
        "L0_gnn_bhh", "L0_ffn_router_w", "L0_ffn_router_b", "L0_ffn_W1", "L0_ffn_b1", "L0_ffn_W2", "L0_ffn_b2"]


def kernel(**inputs):
    import numpy as _np
    import concourse.bacc as _bacc
    from concourse import mybir as _mybir
    from concourse.bass_utils import run_bass_kernel_spmd as _run

    nc = _bacc.Bacc("TRN2", target_bir_lowering=False, num_devices=1)
    arrays, args = {}, []
    for name in _INS:
        a = _np.ascontiguousarray(inputs[name])
        arrays[f"in_{name}_dram"] = a
        args.append(nc.dram_tensor(f"in_{name}_dram", a.shape, _mybir.dt.from_np(a.dtype), kind="ExternalInput").ap())
    shape = arrays["in_x_dram"].shape
    args.append(nc.dram_tensor("out_0_dram", shape, _mybir.dt.float32, kind="ExternalOutput").ap())
    gnn_lstm_moe(nc, *args)
    r = _run(nc, [arrays], core_ids=[0])
    return r.results[0]["out_0_dram"]
```

```python
from contextlib import ExitStack

import concourse.bass as bass
from concourse import mybir

F32 = mybir.dt.float32
F32R = mybir.dt.float32r
BF16 = mybir.dt.bfloat16
ALU = mybir.AluOpType
ACT = mybir.ActivationFunctionType
AX = mybir.AxisListType

P = 128
GB = 4
HALF = 512
EPS = 1e-5
UNPICKED = -1e30

I_, F_, G_, O_ = 0, 1, 2, 3


def lstm_steps(max_p):
    steps = [(1, 0, 0), (1, 0, 1)]
    for p in range(2, max_p + 1):
        steps += [(p, s, None) for s in range(p)]
    return steps


def gates_of(s):
    return (I_, G_, O_) if s == 0 else (I_, G_, F_, O_)


STEPS = lstm_steps(4)
NSTEP = len(STEPS)
TILE = {}
for _n, (_p, _s, _c) in enumerate(STEPS):
    for _q in gates_of(_s):
        TILE[_n, _q] = len(TILE)
NTILE = len(TILE)


def tile_before(n, gate):
    for m in range(n - 1, -1, -1):
        if (m, gate) in TILE:
            return 0, TILE[m, gate]
    return 1, max(t for (m, q), t in TILE.items() if q == gate)


STAGE_GROUP = {"G": 1, "A": -1, "B": -1, "T": -2}
NEQ = 8
FILL = {
    "PE": [
        "T:m1 T:q0 | T:m2",
        "T:m3 T:q1 T:q2 | T:m4 A:t T:m5 T:q3",
        "| T:q4 A:x T:m6 T:q5 T:m7 A:l",
        "G:y0 T:q6 T:q7 | A:o T:e A:m0 B:t",
        "A:m1 G:y1 | G:w0",
        "A:m2 A:q0 B:x A:q1 A:m3 |",
        "A:m4 G:w1 A:q2 A:q3 | A:m5 B:l A:m6",
        "A:q4 G:z0 |",
        "A:m7 B:o | G:z1",
        "A:q5 B:m0 A:q6 G:a0 | A:q7",
        "G:a1 A:e |",
    ],
    "ACT": [
        "T:m1 T:m2 |",
        "T:m3 | G:c T:m4",
        "T:m5 | A:x G:f T:m6 T:m7",
        "G:y0 | T:q7 A:o",
        "A:m0 A:m1 | G:y1 G:w0",
        "| A:m2 B:x A:m3",
        "G:w1 A:m4 |",
        "A:m5 | G:z0 A:m6",
        "B:o | G:z1",
        "| A:m7 G:a0 A:q7",
        "G:a1 B:m0 |",
    ],
    "DVE": [
        "G:s T:m1 T:m2 |",
        "G:c T:m3 | A:t",
        "T:m4 T:m5 G:f A:n | A:x T:m6 T:m7 A:l",
        "G:y0 | T:e B:t",
        "A:m0 | A:m1 G:y1 B:n G:w0",
        "A:m2 | A:m3 B:x",
        "G:w1 A:m4 | B:l",
        "A:m5 | G:z0",
        "| A:m6 G:z1",
        "A:m7 | G:a0",
        "G:a1 | B:m0 A:e",
    ],
}
FILL = {eng: [[[(u[0], u[2:]) for u in part.split()] for part in slot.split("|")] for slot in slots]
        for eng, slots in FILL.items()}
FLAT = {eng: [u for slot in slots for part in slot for u in part] for eng, slots in FILL.items()}
for _order in FLAT.values():
    _order = [st for st, u in _order if st in "TB"]
    assert _order == sorted(_order, reverse=True)

GNN_UNITS = ["y0", "y1", "w0", "w1", "z0", "z1", "a0", "a1"]
EXP_UNITS = ["t", "x", "l", "o"] + [f"m{k}" for k in range(NEQ)] + ["e"]
UNIT = {"G": {u: n for n, u in enumerate(GNN_UNITS)}}
UNIT["A"] = UNIT["B"] = UNIT["T"] = {u: n for n, u in enumerate(EXP_UNITS)}
NGNN, NEXP = len(GNN_UNITS), len(EXP_UNITS)


def bank_of(stage, unit):
    return 1 + int(unit[1]) % 2 if unit[0] == "m" else 0


BANK_USERS = [(st, u) for st, u in FLAT["PE"] if u in UNIT[st]]


def bank_before(stage, unit, present):
    at = BANK_USERS.index((stage, unit))
    for back in range(3):
        for st, u in reversed(BANK_USERS[:at] if back == 0 else BANK_USERS):
            if bank_of(st, u) == bank_of(stage, unit) and present(st, back):
                return st, u, back
    return None


SETUP = ["adj", "bm0", "wg0", "wg1", "bias"] + [f"ih{p}" for p in range(4)] + \
        [f"hh{p}" for p in range(1, 4)] + ["router", "w1", "w2", "b2"]
SETUP_AT = {name: n + 1 for n, name in enumerate(SETUP)}
SETUP_PE = ["adj", "bm0", "bias"] + [f"ih{p}" for p in range(4)] + [f"hh{p}" for p in range(1, 4)]
SETUP_PE_AT = {name: n + 1 for n, name in enumerate(SETUP_PE)}
SETUP_ACT = ["adj", "wg0", "wg1"] + [f"ih{p}" for p in range(4)] + [f"hh{p}" for p in range(1, 4)] + \
            ["router", "w1", "w2"]
SETUP_ACT_AT = {name: n + 1 for n, name in enumerate(SETUP_ACT)}


def gnn_lstm_moe(nc, x, adj, Wg0, bg0, Wg1, bg1, Wih, Whh, bih, bhh, router_w, router_b, W1, b1, W2, b2, out):
    B, T, D = x.shape
    NG = B // GB
    TOK = GB * T
    KT = T // P
    TILES = TOK // P
    E, _, HE = W1.shape
    EQ = E * HE // P
    EPT = P // HE
    MP = Wih.shape[0]
    assert D == P and KT == 2 and TILES == 8 and EQ == 8 and MP == 4 and TOK == 2 * HALF and E == 32

    ctx = ExitStack()
    with ctx:
        def sb(name, shape, dt=F32):
            return ctx.enter_context(nc.sbuf_tensor(name, shape, dt))

        def sem(name):
            return ctx.enter_context(nc.semaphore(name))

        ident = sb("ident", [P, P])
        ident16 = sb("ident16", [P, P], BF16)
        ones_r = sb("ones_r", [P, P], F32R)
        adjT_hi, adjT_lo = (sb(f"adjT_{v}", [P, KT, T], F32R) for v in ("hi", "lo"))
        wg_hi, wg_lo = (sb(f"wg_{v}", [P, 2, P], F32R) for v in ("hi", "lo"))
        wih_hi, wih_lo = (sb(f"wih_{v}", [P, MP, 4 * P], F32R) for v in ("hi", "lo"))
        whh_hi, whh_lo = (sb(f"whh_{v}", [P, MP - 1, 4 * P], F32R) for v in ("hi", "lo"))
        w1_hi, w1_lo = (sb(f"w1_{v}", [P, E * HE], F32R) for v in ("hi", "lo"))
        w2_hi, w2_lo = (sb(f"w2_{v}", [P, EQ, P], F32R) for v in ("hi", "lo"))
        rT_hi, rT_lo = (sb(f"rT_{v}", [P, E], F32R) for v in ("hi", "lo"))
        wg_raw = sb("wg_raw", [P, 2, P])
        adj_raw = sb("adj_raw", [P, KT, T])
        r_raw = sb("r_raw", [E, P])
        b_raw = sb("b_raw", [4 * MP, 2, P])
        bsum = sb("bsum", [4 * MP, P])
        rb = sb("rb", [P, E])
        bg0col = sb("bg0col", [P, 1])
        bg1row = sb("bg1row", [P, P])
        bm0 = sb("bm0", [P, T])
        gbias = sb("gbias", [P, 4 * MP])
        b1_raw = sb("b1_raw", [3 * E, HE])
        b2_raw = sb("b2_raw", [3 * E, P])
        b1_rest = sb("b1_rest", [3 * E, 2, HE])
        b2_rest = sb("b2_rest", [3 * E, 2, P])
        b1_part = sb("b1_part", [3 * E, 3, HE], BF16)
        b2_part = sb("b2_part", [3 * E, 3, P], BF16)
        b1_sel = sb("b1_sel", [3 * E, EQ, EPT, HE], BF16)
        b2_sel = sb("b2_sel", [3 * E, P], BF16)
        rank = sb("rank", [P, E])
        half_neg = sb("half_neg", [P, TILES])

        pause = sb("pause", [P, 1])

        x_nat = sb("x_nat", [P, TILES, P])
        HT = TILES // 2
        st1 = sb("st1", [P, TILES, 6])
        mv1 = sb("mv1", [P, TILES, 2])
        ve1 = sb("ve1", [P, TILES])
        rs1 = sb("rs1", [P, TILES])
        mrs1 = sb("mrs1", [P, TILES])
        xn = sb("xn", [P, TILES, P])
        xn_hi, xn_lo = (sb(f"xn_{v}", [P, TILES, P], F32R) for v in ("hi", "lo"))
        yz_hi, yz_lo = (sb(f"yz_{v}", [P, 2, HALF], F32R) for v in ("hi", "lo"))
        gf = sb("gf", [P, 2, HALF])
        h1_hi, h1_lo = (sb(f"h1_{v}", [P, 2, HALF], F32R) for v in ("hi", "lo"))
        hin_hi, hin_lo = (sb(f"hin_{v}", [P, TOK], F32R) for v in ("hi", "lo"))
        hb_hi, hb_lo = (sb(f"hb_{v}", [P, T, GB], F32R) for v in ("hi", "lo"))
        gact = sb("gact", [P, 2, 4, HALF])
        cell = sb("cell", [P, HALF])
        ig = sb("ig", [P, HALF])
        fc = sb("fc", [P, HALF])
        tc = sb("tc", [P, HALF])
        hf = sb("hf", [P, HALF])
        hs_hi, hs_lo = (sb(f"hs_{v}", [P, HALF], F32R) for v in ("hi", "lo"))
        hfull = sb("hfull", [P, GB, T])
        x_res = sb("x_res", [P, TILES, P])
        x2 = sb("x2", [P, TILES, P])
        st2 = sb("st2", [P, TILES, 6])
        mv2 = sb("mv2", [P, TILES, 2])
        ve2 = sb("ve2", [P, TILES])
        rs2 = sb("rs2", [P, TILES])
        xn2 = sb("xn2", [P, TILES, P])
        xT_hi, xT_lo = (sb(f"xT_{v}", [P, TOK], F32R) for v in ("hi", "lo"))
        lg = sb("lg", [P, TILES, E])
        lmax = sb("lmax", [P, TILES, 1])
        cand = sb("cand", [P, TILES, E])
        best = sb("best", [P, TILES, 1])
        oh3 = sb("oh3", [P, TILES, 3 * E], BF16)
        ohT = sb("ohT", [3 * E, TOK], BF16)
        hm_hi, hm_lo = (sb(f"hm_{v}", [P, 2, HALF], F32R) for v in ("hi", "lo"))
        orel = sb("orel", [P, HALF])
        obuf = sb("obuf", [P, TILES, P])
        wih_raw = gact[:, 0, :, :].rearrange("p q (r c) -> p (q r) c", c=P)
        whh_raw = gact[:, 1, :, :].rearrange("p q (r c) -> p (q r) c", c=P)
        w1_raw = obuf[:, :, :].rearrange("p a b -> p (a b)")
        w2_raw = xn2

        gate_ps = [ctx.enter_context(nc.psum_tensor(f"gate_ps{q}", [P, HALF], F32)) for q in range(4)]
        fill_ps = [ctx.enter_context(nc.psum_tensor(f"fill_ps{q}", [P, HALF], F32)) for q in range(3)]
        acc_ps = ctx.enter_context(nc.psum_tensor("acc_ps", [P, HALF], F32))

        adj_loaded, w_loaded = sem("adj_loaded"), sem("w_loaded")
        xnat_loaded, xres_loaded = sem("xnat_loaded"), sem("xres_loaded")
        const_made = sem("const_made")
        b1_split = sem("b1_split")
        b1_sel_made = sem("b1_sel_made")
        setup_pe, setup_hi, setup_done = sem("setup_pe"), sem("setup_hi"), sem("setup_done")
        dve_tmp = sem("dve_tmp")
        ln1_stat, ln1_aggr, ln1_var, ln1_rstd = sem("ln1_stat"), sem("ln1_aggr"), sem("ln1_var"), sem("ln1_rstd")
        ln1_shift = sem("ln1_shift")
        ln1_read, ln1_hi, xn_ready = sem("ln1_read"), sem("ln1_hi"), sem("xn_ready")
        gnn_biased, gnn_hi = sem("gnn_biased"), sem("gnn_hi")
        gate_ready, gate_done = sem("gate_ready"), sem("gate_done")
        prod_ready, cell_ready, tanh_ready = sem("prod_ready"), sem("cell_ready"), sem("tanh_ready")
        hf_ready, h_hi_ready, h_lo_ready = sem("hf_ready"), sem("h_hi_ready"), sem("h_lo_ready")
        hfull_ready = sem("hfull_ready")

        def by_half(name):
            a, b = sem(name + "_a"), sem(name + "_b")
            return {"A": a, "B": b, "T": b}

        ready, drained = by_half("ready"), by_half("drained")
        ready["G"], drained["G"] = sem("ready_g"), sem("drained_g")
        ln2_stat, ln2_aggr, ln2_var, ln2_rstd = by_half("ln2_stat"), by_half("ln2_aggr"), by_half("ln2_var"), by_half("ln2_rstd")
        xn2_ready, xT_hi_ready, oh_step = by_half("xn2_ready"), by_half("xT_hi_ready"), by_half("oh_step")
        hm_hi_ready, w2_used = by_half("hm_hi_ready"), by_half("w2_used")
        acc_ready, orel_ready = by_half("acc_ready"), by_half("orel_ready")
        stored = by_half("stored")

        x_v = x.rearrange("(n b) (k s) d -> n s (b k) d", b=GB, s=P)
        out_v = out.rearrange("(n b) (k s) d -> n s (b k) d", b=GB, s=P)

        def columns(n):
            p, s, chunk = STEPS[n]
            return HALF if p == 1 else (T // p) * GB

        def tokens(hi_or_lo, n, last=False):
            p, s, chunk = STEPS[n]
            if p == 1:
                v = hi_or_lo if last is False else hi_or_lo[:, :, :].rearrange("p t b -> p (t b)")
                return v[:, chunk * HALF:(chunk + 1) * HALF]
            a = p - 1 if last else s
            return hi_or_lo[:, a:a + p * (T // p - 1) + 1:p, :]

        def as_tokens(flat, n):
            return flat if STEPS[n][0] == 1 else flat.rearrange("p (t b) -> p t b", b=GB)

        def is_last(n):
            p, s, _ = STEPS[n]
            return s == p - 1

        def wait(eng, s, g, per_group, value):
            if isinstance(g, int):
                if per_group * g + value > 0:
                    eng.wait_ge(s, per_group * g + value)
            else:
                eng.wait_ge(s, g * per_group + value)

        def per_group(stage):
            return NGNN if stage == "G" else NEXP

        def is_ready(eng, stage, g, unit):
            wait(eng, ready[stage], g, per_group(stage), UNIT[stage][unit] + 1)

        def is_drained(eng, stage, g, unit):
            wait(eng, drained[stage], g, per_group(stage), UNIT[stage][unit] + 1)

        def x2_is_taken(eng, g):
            if not (isinstance(g, int) and g < 0):
                is_drained(eng, "A", g, "t")
                is_drained(eng, "B", g, "t")

        def exists(stage, i):
            return not isinstance(i, int) or 0 <= i + STAGE_GROUP[stage] < NG

        def bank_is_free(eng, i, stage, unit):
            at = bank_before(stage, unit, lambda st, back: exists(st, i - back))
            if at is not None:
                st, u, back = at
                is_drained(eng, st, i - back + STAGE_GROUP[st], u)

        def fill(eng, slot, part, i, do):
            for stage, unit in FILL[eng][slot][part]:
                if exists(stage, i):
                    do(i, stage, i + STAGE_GROUP[stage], unit)

        def half_of(stage):
            return 0 if stage == "A" else 1

        block = ctx.enter_context(nc.Block())

        def run(eng, body):
            for i in range(-1, 3):
                body(i)
            with eng.Fori(3, NG - 1) as i:
                body(i)
            for i in range(NG - 1, NG + 2):
                body(i)

        def has_lstm(i):
            return not isinstance(i, int) or 0 <= i < NG

        @block.sync
        def _(sp):
            sp.dma_start(adj_raw[:, :, :], adj.rearrange("(k t) s -> t k s", t=P)).then_inc(adj_loaded, 16)
            sp.dma_start(x_nat[:, :, :], x_v[0]).then_inc(xnat_loaded, 16)
            loads = [
                (wg_raw[:, 0, :], Wg0), (wg_raw[:, 1, :], Wg1),
                (bg0col[:, :], bg0.rearrange("(h a) -> h a", a=1)),
                (bg1row[:, :], bg1.partition_broadcast(P)),
                (b_raw[:, 0, :], bih.rearrange("p (q h) -> (p q) h", h=P)),
                (b_raw[:, 1, :], bhh.rearrange("p (q h) -> (p q) h", h=P)),
                (wih_raw, Wih.rearrange("p (q a) h -> a (p q) h", a=P)),
                (whh_raw, Whh.rearrange("p (q a) h -> a (p q) h", a=P)),
                (r_raw[:, :], router_w), (rb[:, :], router_b.partition_broadcast(P)),
                (w1_raw.rearrange("p (e h) -> p e h", h=HE), W1.rearrange("e d h -> d e h")),
                (w2_raw[:, :, :], W2.rearrange("(q e) h d -> (e h) q d", e=EPT)),
            ]
            loads += [(b1_raw[E * r:E * r + E, :], b1) for r in range(3)]
            loads += [(b2_raw[E * r:E * r + E, :], b2) for r in range(3)]
            for dst, src in loads:
                sp.dma_start(dst, src).then_inc(w_loaded, 16)
            assert len(loads) == N_LOADS

            def body(i):
                if exists("G", i) and not (isinstance(i, int) and i == -1):
                    wait(sp, ln1_read, i + 1, 1, 0)
                    sp.dma_start(x_nat[:, :, :], x_v[i + 1]).then_inc(xnat_loaded, 16)
                if exists("A", i):
                    x2_is_taken(sp, i - 2)
                    sp.dma_start(x_res[:, :, :], x_v[i - 1]).then_inc(xres_loaded, 16)

            run(sp, body)

        @block.gpsimd
        def _(pool):
            nc.gpsimd.memset(ident[:, :], 0.0).then_inc(const_made, 1)
            nc.gpsimd.memset(ident16[:, :], 0.0).then_inc(const_made, 1)
            nc.gpsimd.memset(ones_r[:, :].bitcast(F32), 1.0).then_inc(const_made, 1)
            nc.gpsimd.memset(half_neg[:, :], -0.5).then_inc(const_made, 1)
            nc.gpsimd.iota(rank[:, :], pattern=[[-1, E]], base=E, channel_multiplier=0,
                           allow_small_or_imprecise_dtypes=True).then_inc(const_made, 1)
            pool.wait_ge(const_made, 5)
            for m in (ident, ident16):
                nc.gpsimd.affine_select(out=m[:, :], in_=m[:, :], compare_op=ALU.not_equal, fill=1.0, base=0,
                                        pattern=[[-1, P]], channel_multiplier=1).then_inc(const_made, 1)

            def power(g, ve, rs, a, b, var, rstd):
                wait(pool, var, g, 1, 1)
                nc.gpsimd.tensor_tensor(rs[:, a:b], ve[:, a:b], half_neg[:, a:b], ALU.pow).then_inc(rstd, 1)

            def unit(i, stage, g, u):
                if (stage, u) == ("G", "s"):
                    power(g, ve1, rs1, 0, TILES, ln1_var, ln1_rstd)
                elif (stage, u) == ("G", "f"):
                    wait(pool, ln1_hi, g, 1, 1)
                    nc.gpsimd.tensor_tensor(xn_lo[:, :, :], xn[:, :, :], xn_hi[:, :, :].bitcast(F32), ALU.subtract)\
                        .then_inc(xn_ready, 1)
                elif stage in "AB" and u == "t":
                    a = half_of(stage) * HT
                    power(g, ve2, rs2, a, a + HT, ln2_var[stage], ln2_rstd[stage])
                elif stage in "ABT" and u == "e":
                    is_drained(pool, stage, g, "e")
                    a = half_of(stage) * HT
                    pool.dma_start(out_v[g][:, a:a + HT, :], obuf[:, a:a + HT, :]).then_inc(stored[stage], 16)

            def whole_h(g):
                wait(pool, h_lo_ready, g, NSTEP, NSTEP)
                if not (isinstance(g, int) and g == 0):
                    is_ready(pool, "A", g - 1, "t")
                    is_ready(pool, "B", g - 1, "t")
                o = hfull[:, :, :].rearrange("p b t -> p t b")
                nc.gpsimd.tensor_tensor(o, hb_hi[:, :, :].bitcast(F32), hb_lo[:, :, :].bitcast(F32), ALU.add)\
                    .then_inc(hfull_ready, 1)

            def selector():
                pool.wait_ge(b1_split, 1)
                pool.wait_ge(xn_ready, 1)
                for r in range(3):
                    if r > 0:
                        pool.wait_ge(b1_sel_made, r)
                    src = b1_part[E * r:E * r + E, r, :].unsqueeze(1).to_broadcast([E, E, HE])
                    nc.gpsimd.affine_select(
                        out=b1_sel[E * r:E * r + E, :, :, :].rearrange("p q e h -> p (q e) h"), in_=src,
                        compare_op=ALU.is_equal, fill=UNPICKED if r == 0 else 0.0, base=0,
                        pattern=[[-1, E], [0, HE]], channel_multiplier=1).then_inc(b1_sel_made, 1)
                pool.wait_ge(b1_sel_made, 3)

            def body(i):
                for n in range(NSTEP):
                    for part in range(2):
                        fill("DVE", n, part, i, unit)
                if has_lstm(i):
                    whole_h(i)
                if isinstance(i, int) and i == -1:
                    selector()

            run(pool, body)
            for stage in "AB":
                pool.wait_ge(stored[stage], 16 * NG)

        @block.tensor
        def _(pe):
            def three(o, w_hi, w_lo, r_hi, r_lo, start, stop):
                nc.tensor.matmul(o, w_hi, r_hi, start=start, stop=False)
                nc.tensor.matmul(o, w_lo, r_hi, start=False, stop=False)
                return nc.tensor.matmul(o, w_hi, r_lo, start=False, stop=stop)

            pe.wait_ge(const_made, 7)
            pe.wait_ge(adj_loaded, 16)
            for k in range(KT):
                for t in range(KT):
                    mm = nc.tensor.transpose(fill_ps[0][:, k * T + t * P:k * T + t * P + P],
                                             adj_raw[:, t, k * P:k * P + P], ident[:, :])
            mm.then_inc(setup_pe, 1)
            pe.wait_ge(setup_done, SETUP_AT["adj"])
            for k in range(KT):
                nc.tensor.matmul(fill_ps[1][:, 0:T], ones_r[:, :], adjT_hi[:, k, :], start=(k == 0), stop=False)
                mm = nc.tensor.matmul(fill_ps[1][:, 0:T], ones_r[:, :], adjT_lo[:, k, :], start=False, stop=(k == KT - 1))
            mm.then_inc(setup_pe, 1)
            pe.wait_ge(w_loaded, 16 * N_LOADS)
            pe.wait_ge(dve_tmp, 1)
            nc.tensor.transpose(fill_ps[2][:, 0:E], r_raw[:, :], ident[0:E, 0:E])
            nc.tensor.transpose(fill_ps[2][:, E:E + 4 * MP], bsum[:, :], ident[0:4 * MP, 0:4 * MP])\
                .then_inc(setup_pe, 1)
            for n, name in enumerate(SETUP_PE[3:]):
                raw, p = (wih_raw, int(name[2])) if name[0] == "i" else (whh_raw, int(name[2]))
                if n >= 4:
                    pe.wait_ge(setup_done, SETUP_AT[SETUP_PE[3 + n - 4]])
                for q in range(4):
                    mm = nc.tensor.transpose(gate_ps[n % 4][:, q * P:q * P + P], raw[:, 4 * p + q, :], ident[:, :])
                mm.then_inc(setup_pe, 1)

            def gnn(i, g, unit):
                kind, u = unit[0], int(unit[1])
                bank_is_free(pe, i, "G", unit)
                if kind == "y":
                    wait(pe, xn_ready, g, 1, 1)
                    for bb in range(2):
                        o = fill_ps[0][:, bb * T:bb * T + T]
                        for k in range(KT):
                            j = (2 * u + bb) * KT + k
                            mm = three(o, xn_hi[:, j, :], xn_lo[:, j, :], adjT_hi[:, k, :], adjT_lo[:, k, :],
                                       k == 0, k == KT - 1)
                elif kind == "w":
                    is_drained(pe, "G", g, f"y{u}")
                    mm = three(fill_ps[0][:, :], wg_hi[:, 0, :], wg_lo[:, 0, :], yz_hi[:, u, :], yz_lo[:, u, :], True, True)
                elif kind == "z":
                    is_drained(pe, "G", g, f"w{u}")
                    for j in range(2 * KT):
                        c = slice(j * P, j * P + P)
                        mm = three(fill_ps[0][:, c], h1_hi[:, u, c], h1_lo[:, u, c], wg_hi[:, 1, :], wg_lo[:, 1, :],
                                   True, True)
                else:
                    is_drained(pe, "G", g, f"z{u}")
                    for bb in range(2):
                        o = fill_ps[0][:, bb * T:bb * T + T]
                        for k in range(KT):
                            c = slice((bb * KT + k) * P, (bb * KT + k) * P + P)
                            mm = three(o, yz_hi[:, u, c], yz_lo[:, u, c], adjT_hi[:, k, :], adjT_lo[:, k, :],
                                       k == 0, k == KT - 1)
                mm.then_inc(ready["G"], 1)

            def gates_x(g, n):
                p, s, _ = STEPS[n]
                N = columns(n)
                if p == 1:
                    is_drained(pe, "G", g, "a1")
                    r_hi, r_lo = tokens(hin_hi, n), tokens(hin_lo, n)
                else:
                    r_hi, r_lo = tokens(hb_hi, n), tokens(hb_lo, n)
                    if s == 0:
                        wait(pe, h_lo_ready, g, NSTEP, n)
                for q in gates_of(s):
                    back, t = tile_before(n, q)
                    wait(pe, gate_done, g, NTILE, t + 1 - back * NTILE)
                    c = slice(q * P, q * P + P)
                    mm = three(as_tokens(gate_ps[q][:, 0:N], n), wih_hi[:, p - 1, c], wih_lo[:, p - 1, c],
                               r_hi, r_lo, True, s == 0)
                    if s == 0:
                        mm.then_inc(gate_ready, 1)

            def gates_h(g, n):
                p, s, _ = STEPS[n]
                N = columns(n)
                wait(pe, h_hi_ready, g, NSTEP, n)
                for q in gates_of(s):
                    c = slice(q * P, q * P + P)
                    nc.tensor.matmul(gate_ps[q][:, 0:N], whh_hi[:, p - 2, c], hs_hi[:, 0:N], start=False, stop=False)
                    nc.tensor.matmul(gate_ps[q][:, 0:N], whh_lo[:, p - 2, c], hs_hi[:, 0:N], start=False, stop=False)
                wait(pe, h_lo_ready, g, NSTEP, n)
                for q in gates_of(s):
                    nc.tensor.matmul(gate_ps[q][:, 0:N], whh_hi[:, p - 2, q * P:q * P + P], hs_lo[:, 0:N],
                                     start=False, stop=True).then_inc(gate_ready, 1)

            def second_product(stage, g, q):
                if q == 0:
                    if stage == "A":
                        if not (isinstance(g, int) and g == 0):
                            wait(pe, orel_ready["B"], g, 1, 0)
                    else:
                        wait(pe, orel_ready["A"], g, 1, 1)
                is_drained(pe, stage, g, f"m{q}")
                three(acc_ps[:, :], w2_hi[:, q, :], w2_lo[:, q, :], hm_hi[:, q % 2, :], hm_lo[:, q % 2, :],
                      q == 0, False).then_inc(w2_used[stage], 1)
                if q == EQ - 1:
                    c = slice(half_of(stage) * HALF, half_of(stage) * HALF + HALF)
                    nc.tensor.matmul(acc_ps[:, :], b2_sel[:, :], ohT[:, c], start=False, stop=True)\
                        .then_inc(acc_ready[stage], 1)

            def expert(i, stage, g, unit):
                if unit[0] == "q":
                    second_product(stage, g, int(unit[1]))
                    return
                h = half_of(stage)
                o = fill_ps[bank_of(stage, unit)]
                c = slice(h * HALF, h * HALF + HALF)
                bank_is_free(pe, i, stage, unit)
                if unit == "t":
                    wait(pe, hfull_ready, g, 1, 1)
                    cols = hfull[:, :, :].rearrange("p b t -> p (b t)")
                    for j in range(HT):
                        at = (HT * h + j) * P
                        mm = nc.tensor.transpose(o[:, j * P:j * P + P], cols[:, at:at + P], ident[:, :])
                elif unit == "x":
                    wait(pe, xn2_ready[stage], g, 1, 1)
                    for j in range(HT):
                        mm = nc.tensor.transpose(o[:, j * P:j * P + P], xn2[:, HT * h + j, :], ident[:, :])
                elif unit == "l":
                    is_drained(pe, stage, g, "x")
                    for j in range(HT):
                        t = slice(h * HALF + j * P, h * HALF + j * P + P)
                        mm = three(o[:, j * E:j * E + E], xT_hi[:, t], xT_lo[:, t], rT_hi[:, :], rT_lo[:, :], True, True)
                elif unit == "o":
                    wait(pe, oh_step[stage], g, 7, 7)
                    o16 = o[:, :].bitcast(BF16)
                    for j in range(HT):
                        mm = nc.tensor.transpose(o16[0:3 * E, j * P:j * P + P], oh3[:, HT * h + j, :], ident16[:, :])
                elif unit[0] == "m":
                    q = int(unit[1])
                    if q == 0:
                        is_drained(pe, stage, g, "o")
                    nc.tensor.matmul(o[:, :], b1_sel[:, q, :, :].rearrange("p e h -> p (e h)"), ohT[:, c],
                                     start=True, stop=False)
                    mm = three(o[:, :], w1_hi[:, q * P:q * P + P], w1_lo[:, q * P:q * P + P], xT_hi[:, c], xT_lo[:, c],
                               False, True)
                else:
                    wait(pe, orel_ready[stage], g, 1, 1)
                    for j in range(HT):
                        mm = nc.tensor.transpose(o[:, j * P:j * P + P], orel[:, j * P:j * P + P], ident[:, :])
                mm.then_inc(ready[stage], 1)

            def unit(i, stage, g, u):
                if stage == "G":
                    gnn(i, g, u)
                else:
                    expert(i, stage, g, u)

            pe.wait_ge(setup_done, SETUP_AT["wg1"])

            def body(i):
                for n in range(NSTEP):
                    if has_lstm(i):
                        if STEPS[n][1] == 0:
                            gates_x(i, n)
                        else:
                            gates_h(i, n)
                    fill("PE", n, 0, i, unit)
                    if has_lstm(i) and n + 1 < NSTEP and STEPS[n + 1][1] > 0:
                        gates_x(i, n + 1)
                    fill("PE", n, 1, i, unit)
                if isinstance(i, int) and i == -1:
                    pe.wait_ge(setup_done, SETUP_AT["b2"])
                    pe.wait_ge(b1_sel_made, 3)

            run(pe, body)

        @block.scalar
        def _(act):
            def hi_of(dst, src):
                return nc.scalar.copy(dst, src)

            act.wait_ge(setup_pe, SETUP_PE_AT["adj"])
            hi_of(adjT_hi[:, :, :].rearrange("p k t -> p (k t)"), fill_ps[0][:, :]).then_inc(setup_hi, 1)
            act.wait_ge(w_loaded, 16 * N_LOADS)
            for n in range(2):
                hi_of(wg_hi[:, n, :], wg_raw[:, n, :]).then_inc(setup_hi, 1)
            for n, name in enumerate(SETUP_PE[3:]):
                act.wait_ge(setup_pe, SETUP_PE_AT[name])
                dst = wih_hi[:, n, :] if n < 4 else whh_hi[:, n - 4, :]
                hi_of(dst, gate_ps[n % 4][:, :]).then_inc(setup_hi, 1)
            act.wait_ge(setup_pe, SETUP_PE_AT["bias"])
            hi_of(rT_hi[:, :], fill_ps[2][:, 0:E]).then_inc(setup_hi, 1)
            hi_of(w1_hi[:, :], w1_raw).then_inc(setup_hi, 1)
            hi_of(w2_hi[:, :, :], w2_raw[:, :, :]).then_inc(setup_hi, 1)

            def gnn(g, unit):
                if unit == "c":
                    if not (isinstance(g, int) and g == 0):
                        is_drained(act, "G", g - 1, "y1")
                    wait(act, ln1_shift, g, 1, 1)
                    for j in range(TILES):
                        a = nc.scalar.activation(xn[:, j, :], x_nat[:, j, :], ACT.Identity, bias=mrs1[:, j:j + 1],
                                                 scale=rs1[:, j:j + 1])
                    a.then_inc(ln1_read, 1)
                    return
                if unit == "f":
                    wait(act, ln1_read, g, 1, 1)
                    hi_of(xn_hi[:, :, :], xn[:, :, :]).then_inc(ln1_hi, 1)
                    return
                kind, u, n = unit[0], int(unit[1]), UNIT["G"][unit]
                if kind in "wz":
                    wait(act, gnn_biased, g, 4, n - 1)
                    if kind == "w":
                        a = nc.scalar.activation(h1_hi[:, u, :], gf[:, u, :], ACT.Relu)
                    else:
                        a = hi_of(yz_hi[:, u, :], gf[:, u, :])
                else:
                    is_ready(act, "G", g, unit)
                    if kind == "y":
                        a = hi_of(yz_hi[:, u, :], fill_ps[0][:, :])
                    else:
                        o = hin_hi[:, :].rearrange("p (t b) -> p b t", b=GB)[:, 2 * u:2 * u + 2, :]
                        a = nc.scalar.activation(o, fill_ps[0][:, :].rearrange("p (b t) -> p b t", b=2), ACT.Relu)
                a.then_inc(gnn_hi, 1)

            def gates(g, n):
                p, s, _ = STEPS[n]
                N = columns(n)
                if n == 0:
                    wait(act, h_hi_ready, g, NSTEP, 0)
                for q in gates_of(s):
                    wait(act, gate_ready, g, NTILE, TILE[n, q] + 1)
                    nc.scalar.activation(gact[:, n % 2, q, 0:N], gate_ps[q][:, 0:N], ACT.Tanh if q == G_ else ACT.Sigmoid,
                                         bias=gbias[:, 4 * (p - 1) + q:4 * (p - 1) + q + 1]).then_inc(gate_done, 1)

            def cell_tanh(g, n):
                N = columns(n)
                wait(act, cell_ready, g, NSTEP, n + 1)
                nc.scalar.activation(tc[:, 0:N], cell[:, 0:N], ACT.Tanh).then_inc(tanh_ready, 1)

            def expert(stage, g, unit):
                h = half_of(stage)
                c = slice(h * HALF, h * HALF + HALF)
                o = fill_ps[bank_of(stage, unit)]
                if unit == "x":
                    is_ready(act, stage, g, unit)
                    hi_of(xT_hi[:, c], o[:, :]).then_inc(xT_hi_ready[stage], 1)
                elif unit == "o":
                    is_ready(act, stage, g, unit)
                    nc.scalar.copy(ohT[:, c], o[:, :].bitcast(BF16)[0:3 * E, 0:HALF]).then_inc(drained[stage], 1)
                elif unit[0] == "m":
                    q = int(unit[1])
                    if q > 1:
                        wait(act, w2_used[stage], g, EQ, q - 1)
                    is_ready(act, stage, g, unit)
                    nc.scalar.activation(hm_hi[:, q % 2, :], o[:, :], ACT.Relu).then_inc(hm_hi_ready[stage], 1)
                elif unit == "q7":
                    wait(act, acc_ready[stage], g, 1, 1)
                    nc.scalar.activation(orel[:, :], acc_ps[:, :], ACT.Relu).then_inc(orel_ready[stage], 1)

            def unit(i, stage, g, u):
                if stage == "G":
                    gnn(g, u)
                else:
                    expert(stage, g, u)

            def body(i):
                for n in range(NSTEP):
                    if has_lstm(i):
                        gates(i, n)
                    fill("ACT", n, 0, i, unit)
                    if has_lstm(i):
                        cell_tanh(i, n)
                    fill("ACT", n, 1, i, unit)
                if isinstance(i, int) and i == -1:
                    act.wait_ge(setup_done, SETUP_AT["bias"])

            run(act, body)

        @block.vector
        def _(dve):
            links = [0]

            def link(ins):
                links[0] += 1
                ins.then_inc(dve_tmp, 1)
                dve.wait_ge(dve_tmp, links[0])

            def lo_of(dst, src, hi, op0=ALU.max, scalar=None):
                if scalar is None:
                    return nc.vector.tensor_tensor(dst, src, hi.bitcast(F32), ALU.subtract)
                return nc.vector.scalar_tensor_tensor(out=dst, in0=src, scalar=scalar, in1=hi.bitcast(F32), op0=op0,
                                                      op1=ALU.subtract)

            def statistics(g, src, st, mv, ve, a, b, stat, aggr, var):
                for j in range(a, b):
                    last = nc.vector.bn_stats(st[:, j, :], src[:, j, :])
                last.then_inc(stat, 1)
                wait(dve, stat, g, 1, 1)
                nc.vector.memset(pause[:, :], 0.0)
                for j in range(a, b):
                    last = nc.vector.bn_aggr(mv[:, j, :], st[:, j, :])
                last.then_inc(aggr, 1)
                wait(dve, aggr, g, 1, 1)
                nc.vector.tensor_scalar(ve[:, a:b], mv[:, a:b, 1], EPS, None, ALU.add).then_inc(var, 1)

            def gnn(g, unit):
                if unit == "f":
                    return
                if unit == "c":
                    wait(dve, ln1_rstd, g, 1, 1)
                    nc.vector.scalar_tensor_tensor(out=mrs1[:, :], in0=mv1[:, :, 0], scalar=-1.0, in1=rs1[:, :],
                                                   op0=ALU.mult, op1=ALU.mult).then_inc(ln1_shift, 1)
                    return
                if unit == "s":
                    wait(dve, xnat_loaded, g, 16, 16)
                    wait(dve, ln1_read, g, 1, 0)
                    statistics(g, x_nat, st1, mv1, ve1, 0, TILES, ln1_stat, ln1_aggr, ln1_var)
                    return
                kind, u, n = unit[0], int(unit[1]), UNIT["G"][unit]
                o = fill_ps[0]
                if kind in "wz":
                    is_ready(dve, "G", g, unit)
                    if kind == "w":
                        bias, shape = bm0[:, :], [P, 2, T]
                    else:
                        bias, shape = bg1row[:, :], [P, 2 * KT, P]
                    view = lambda v: v.rearrange("p (a b) -> p a b", a=shape[1])
                    nc.vector.tensor_tensor(view(gf[:, u, :]), view(o[:, :]), bias.unsqueeze(1).to_broadcast(shape),
                                            ALU.add).then_inc(gnn_biased, 1)
                    wait(dve, gnn_hi, g, NGNN, n + 1)
                    if kind == "w":
                        a = lo_of(h1_lo[:, u, :], gf[:, u, :], h1_hi[:, u, :], scalar=0.0)
                    else:
                        a = lo_of(yz_lo[:, u, :], gf[:, u, :], yz_hi[:, u, :])
                else:
                    wait(dve, gnn_hi, g, NGNN, n + 1)
                    if kind == "y":
                        a = lo_of(yz_lo[:, u, :], o[:, :], yz_hi[:, u, :])
                    else:
                        tb = lambda v: v[:, :].rearrange("p (t b) -> p b t", b=GB)[:, 2 * u:2 * u + 2, :]
                        a = lo_of(tb(hin_lo), o[:, :].rearrange("p (b t) -> p b t", b=2), tb(hin_hi), scalar=0.0)
                a.then_inc(drained["G"], 1)

            def new_cell(g, n):
                p, s, _ = STEPS[n]
                N = columns(n)
                gate = lambda q: gact[:, n % 2, q, 0:N]
                done = lambda q: wait(dve, gate_done, g, NTILE, TILE[n, q] + 1)
                done(G_)
                if s == 0:
                    nc.vector.tensor_tensor(cell[:, 0:N], gate(I_), gate(G_), ALU.mult).then_inc(cell_ready, 1)
                else:
                    nc.vector.tensor_tensor(ig[:, 0:N], gate(I_), gate(G_), ALU.mult).then_inc(prod_ready, 1)
                    done(F_)
                    nc.vector.tensor_tensor(fc[:, 0:N], gate(F_), cell[:, 0:N], ALU.mult).then_inc(prod_ready, 1)
                    later = [m for m in range(NSTEP) if STEPS[m][1] > 0]
                    wait(dve, prod_ready, g, 2 * len(later), 2 * later.index(n) + 2)
                    nc.vector.tensor_tensor(cell[:, 0:N], ig[:, 0:N], fc[:, 0:N], ALU.add).then_inc(cell_ready, 1)

            def new_h(g, n):
                N = columns(n)
                wait(dve, gate_done, g, NTILE, TILE[n, O_] + 1)
                wait(dve, tanh_ready, g, NSTEP, n + 1)
                if n == 0:
                    wait(dve, hfull_ready, g, 1, 0)
                nc.vector.tensor_tensor(hf[:, 0:N], gact[:, n % 2, O_, 0:N], tc[:, 0:N], ALU.mult).then_inc(hf_ready, 1)
                wait(dve, hf_ready, g, NSTEP, n + 1)
                if is_last(n):
                    hi, lo = tokens(hb_hi, n, last=True), tokens(hb_lo, n, last=True)
                    src = as_tokens(hf[:, 0:N], n)
                else:
                    hi, lo, src = hs_hi[:, 0:N], hs_lo[:, 0:N], hf[:, 0:N]
                nc.vector.tensor_copy(hi, src).then_inc(h_hi_ready, 1)
                wait(dve, h_hi_ready, g, NSTEP, n + 1)
                lo_of(lo, src, hi).then_inc(h_lo_ready, 1)

            def expert(stage, g, unit):
                h = half_of(stage)
                a, b = h * HT, h * HT + HT
                c = slice(h * HALF, h * HALF + HALF)
                o = fill_ps[bank_of(stage, unit)]
                by_tile = o[:, :].rearrange("p (a b) -> p a b", b=P)
                if unit == "t":
                    wait(dve, xres_loaded, g, 16, 16)
                    is_ready(dve, stage, g, unit)
                    nc.vector.tensor_tensor(x2[:, a:b, :], by_tile, x_res[:, a:b, :], ALU.add).then_inc(drained[stage], 1)
                    is_drained(dve, stage, g, unit)
                    statistics(g, x2, st2, mv2, ve2, a, b, ln2_stat[stage], ln2_aggr[stage], ln2_var[stage])
                elif unit == "n":
                    wait(dve, ln2_rstd[stage], g, 1, 1)
                    for j in range(a, b):
                        last = nc.vector.tensor_scalar(xn2[:, j, :], x2[:, j, :], mv2[:, j, 0:1], rs2[:, j:j + 1],
                                                       ALU.subtract, ALU.mult)
                    last.then_inc(xn2_ready[stage], 1)
                elif unit == "x":
                    wait(dve, xT_hi_ready[stage], g, 1, 1)
                    lo_of(xT_lo[:, c], o[:, :], xT_hi[:, c]).then_inc(drained[stage], 1)
                elif unit == "l":
                    is_ready(dve, stage, g, unit)
                    full = [P, HT, E]
                    L, C, M, X = lg[:, a:b, :], cand[:, a:b, :], lmax[:, a:b, :], best[:, a:b, :]
                    logits = o[:, 0:HT * E].rearrange("p (a b) -> p a b", b=E)
                    step = lambda ins: ins.then_inc(oh_step[stage], 1)
                    nc.vector.tensor_tensor(L, logits, rb[:, :].unsqueeze(1).to_broadcast(full), ALU.add)\
                        .then_inc(drained[stage], 1)
                    is_drained(dve, stage, g, unit)
                    step(nc.vector.tensor_reduce(M[:, :, 0], L, AX.X, ALU.max))
                    wait(dve, oh_step[stage], g, 7, 1)
                    step(nc.vector.tensor_tensor(C, L, M.to_broadcast(full), ALU.is_ge))
                    wait(dve, oh_step[stage], g, 7, 2)
                    step(nc.vector.tensor_tensor(C, C, rank[:, :].unsqueeze(1).to_broadcast(full), ALU.mult))
                    wait(dve, oh_step[stage], g, 7, 3)
                    step(nc.vector.tensor_reduce(X[:, :, 0], C, AX.X, ALU.max))
                    wait(dve, oh_step[stage], g, 7, 4)
                    for r in range(3):
                        step(nc.vector.tensor_tensor(oh3[:, a:b, r * E:r * E + E], C, X.to_broadcast(full), ALU.is_equal))
                elif unit[0] == "m":
                    q = int(unit[1])
                    wait(dve, hm_hi_ready[stage], g, EQ, q + 1)
                    lo_of(hm_lo[:, q % 2, :], o[:, :], hm_hi[:, q % 2, :], scalar=0.0).then_inc(drained[stage], 1)
                elif unit == "e":
                    is_ready(dve, stage, g, unit)
                    wait(dve, stored[stage], g, 16, 0)
                    nc.vector.tensor_tensor(obuf[:, a:b, :], by_tile, x2[:, a:b, :], ALU.add).then_inc(drained[stage], 1)

            def unit(i, stage, g, u):
                if stage == "G":
                    gnn(g, u)
                else:
                    expert(stage, g, u)

            dve.wait_ge(setup_hi, SETUP_ACT_AT["adj"])
            lo_of(adjT_lo[:, :, :].rearrange("p k t -> p (k t)"), fill_ps[0][:, :],
                  adjT_hi[:, :, :].rearrange("p k t -> p (k t)")).then_inc(setup_done, 1)
            dve.wait_ge(w_loaded, 16 * N_LOADS)
            link(nc.vector.tensor_tensor(bsum[:, :], b_raw[:, 0, :], b_raw[:, 1, :], ALU.add))
            dve.wait_ge(setup_pe, SETUP_PE_AT["bm0"])
            nc.vector.tensor_scalar(bm0[:, :], fill_ps[1][:, 0:T], bg0col[:, 0:1], None, ALU.mult).then_inc(setup_done, 1)
            for n in range(2):
                dve.wait_ge(setup_hi, SETUP_ACT_AT[f"wg{n}"])
                lo_of(wg_lo[:, n, :], wg_raw[:, n, :], wg_hi[:, n, :]).then_inc(setup_done, 1)
            dve.wait_ge(setup_pe, SETUP_PE_AT["bias"])
            nc.vector.tensor_copy(gbias[:, :], fill_ps[2][:, E:E + 4 * MP]).then_inc(setup_done, 1)
            for n, name in enumerate(SETUP_PE[3:]):
                dve.wait_ge(setup_hi, SETUP_ACT_AT[name])
                hi, lo = (wih_hi[:, n, :], wih_lo[:, n, :]) if n < 4 else (whh_hi[:, n - 4, :], whh_lo[:, n - 4, :])
                lo_of(lo, gate_ps[n % 4][:, :], hi).then_inc(setup_done, 1)
            dve.wait_ge(setup_hi, SETUP_ACT_AT["router"])
            lo_of(rT_lo[:, :], fill_ps[2][:, 0:E], rT_hi[:, :]).then_inc(setup_done, 1)
            dve.wait_ge(setup_hi, SETUP_ACT_AT["w1"])
            lo_of(w1_lo[:, :], w1_raw, w1_hi[:, :]).then_inc(setup_done, 1)
            dve.wait_ge(setup_hi, SETUP_ACT_AT["w2"])
            lo_of(w2_lo[:, :, :], w2_raw[:, :, :], w2_hi[:, :, :]).then_inc(setup_done, 1)
            for raw, rest, part in ((b1_raw, b1_rest, b1_part), (b2_raw, b2_rest, b2_part)):
                src = raw[:, :]
                for r in range(3):
                    link(nc.vector.tensor_copy(part[:, r, :], src))
                    if r < 2:
                        link(nc.vector.tensor_tensor(rest[:, r, :], src, part[:, r, :], ALU.subtract))
                        src = rest[:, r, :]
                if raw is b1_raw:
                    nc.vector.engine_nop().then_inc(b1_split, 1)
            for r in range(3):
                a = nc.vector.tensor_copy(b2_sel[E * r:E * r + E, :], b2_part[E * r:E * r + E, r, :])
            a.then_inc(setup_done, 1)

            def body(i):
                for n in range(NSTEP):
                    if has_lstm(i):
                        new_cell(i, n)
                    fill("DVE", n, 0, i, unit)
                    if has_lstm(i):
                        new_h(i, n)
                    fill("DVE", n, 1, i, unit)

            run(dve, body)


N_LOADS = 18

_INS = ["x", "adj", "L0_gnn_Wg0", "L0_gnn_bg0", "L0_gnn_Wg1", "L0_gnn_bg1", "L0_gnn_Wih", "L0_gnn_Whh", "L0_gnn_bih",
        "L0_gnn_bhh", "L0_ffn_router_w", "L0_ffn_router_b", "L0_ffn_W1", "L0_ffn_b1", "L0_ffn_W2", "L0_ffn_b2"]


def kernel(**inputs):
    import numpy as _np
    import concourse.bacc as _bacc
    from concourse import mybir as _mybir
    from concourse.bass_utils import run_bass_kernel_spmd as _run

    nc = _bacc.Bacc("TRN2", target_bir_lowering=False, num_devices=1)
    arrays, args = {}, []
    for name in _INS:
        a = _np.ascontiguousarray(inputs[name])
        arrays[f"in_{name}_dram"] = a
        args.append(nc.dram_tensor(f"in_{name}_dram", a.shape, _mybir.dt.from_np(a.dtype), kind="ExternalInput").ap())
    shape = arrays["in_x_dram"].shape
    args.append(nc.dram_tensor("out_0_dram", shape, _mybir.dt.float32, kind="ExternalOutput").ap())
    gnn_lstm_moe(nc, *args)
    r = _run(nc, [arrays], core_ids=[0])
    return r.results[0]["out_0_dram"]
```

```python
from contextlib import ExitStack

import concourse.bass as bass
from concourse import mybir

F32 = mybir.dt.float32
F32R = mybir.dt.float32r
BF16 = mybir.dt.bfloat16
ALU = mybir.AluOpType
ACT = mybir.ActivationFunctionType
AX = mybir.AxisListType

P = 128
GB = 4
HALF = 512
EPS = 1e-5
UNPICKED = -1e30

I_, F_, G_, O_ = 0, 1, 2, 3


def lstm_steps(max_p):
    steps = [(1, 0, 0), (1, 0, 1)]
    for p in range(2, max_p + 1):
        steps += [(p, s, None) for s in range(p)]
    return steps


def gates_of(s):
    return (I_, G_, O_) if s == 0 else (I_, G_, F_, O_)


STEPS = lstm_steps(4)
NSTEP = len(STEPS)
TILE = {}
for _n, (_p, _s, _c) in enumerate(STEPS):
    for _q in gates_of(_s):
        TILE[_n, _q] = len(TILE)
NTILE = len(TILE)


def tile_before(n, gate):
    for m in range(n - 1, -1, -1):
        if (m, gate) in TILE:
            return 0, TILE[m, gate]
    return 1, max(t for (m, q), t in TILE.items() if q == gate)


STAGE_GROUP = {"G": 1, "A": -1, "B": -1, "T": -2}
NEQ = 8
FILL = {
    "PE": [
        "T:m2 T:q0 | T:q1 T:m3",
        "T:q2 A:t T:q3 | T:m4 T:m5",
        "T:m6 T:q4 | A:x T:q5 T:m7 A:l",
        "A:o | G:y0 T:q6 T:q7 A:m0 T:e A:m1 B:t",
        "A:q0 G:y1 |",
        "A:m2 G:w0 | A:m3 B:x A:q1",
        "G:w1 A:q2 | A:q3 A:m4 A:m5 B:l A:m6",
        "A:q4 A:m7 G:z0 |",
        "A:q5 B:o | G:z1 B:m0",
        "A:q6 G:a0 |",
        "| G:a1 A:q7 B:m1 A:e",
    ],
    "ACT": [
        "T:m2 | T:m3",
        "| T:m4",
        "T:m5 | T:m6 G:c0 A:x G:f0 T:m7 G:c1",
        "A:o G:y0 | T:q7 A:m0 G:f1 A:m1",
        "| G:y1",
        "A:m2 | G:w0 B:x A:m3",
        "G:w1 A:m4 | A:m5",
        "| G:z0 A:m6",
        "B:o | G:z1",
        "A:m7 | G:a0",
        "G:a1 | A:q7 B:m0 B:m1",
    ],
    "DVE": [
        "G:s0 G:s1 T:m2 | T:m3",
        "G:s2 | A:t T:m4 G:c0 A:u",
        "G:f0 T:m5 A:n | A:x T:m6 T:m7 A:l A:k",
        "G:y0 G:f1 | T:e A:m0 B:t B:u",
        "A:m1 | G:y1 B:n",
        "G:w0 | A:m2 B:x A:m3",
        "G:w1 A:m4 | A:m5 B:l",
        "B:k | G:z0 A:m6",
        "| G:z1",
        "| G:a0 A:m7",
        "G:a1 | A:e B:m0 B:m1",
    ],
}
LAST = {
    "PE": [
        "T:q0 T:m2 | T:m3",
        "A:t T:q1 | T:q2 T:m4 T:m5",
        "T:q3 | A:x",
        "A:l T:q4 T:q5 T:m6 T:m7 A:o T:q6 | T:q7 A:m0 T:e",
        "B:t | A:m1",
        "A:q0 A:m2 | B:x",
        "| A:m3 A:q1 B:l A:m4 A:m5",
        "A:q2 A:q3 |",
        "| B:o A:q4 A:m6",
        "A:m7 A:q5 | A:q6 A:q7 B:m0",
        "| A:e B:m1 B:m2",
    ],
    "ACT": [
        "T:m2 |",
        "T:m3 | T:m4",
        "T:m5 | A:x",
        "T:m6 T:m7 A:o | T:q7 A:m0",
        "| A:m1",
        "A:m2 | B:x",
        "A:m3 |",
        "| A:m4",
        "| A:m5",
        "A:m6 A:m7 B:o | A:q7 B:m0",
        "B:m1 | B:m2",
    ],
    "DVE": [
        "T:m2 |",
        "A:t T:m3 | A:u T:m4",
        "A:n | A:x T:m5",
        "A:l A:k T:m6 T:m7 | T:e A:m0",
        "| B:t B:u",
        "B:n | A:m1 B:x A:m2",
        "A:m3 | B:l",
        "| A:m4 B:k",
        "| A:m5",
        "A:m6 A:m7 | B:m0",
        "A:e B:m1 | B:m2",
    ],
}
FILL, LAST = ({eng: [[[(u[0], u[2:]) for u in part.split()] for part in slot.split("|")] for slot in slots]
               for eng, slots in table.items()} for table in (FILL, LAST))
for _table in (FILL, LAST):
    for _slots in _table.values():
        _order = [st for slot in _slots for part in slot for st, u in part if st in "TB"]
        assert _order == sorted(_order, reverse=True)

GNN_UNITS = ["y0", "y1", "w0", "w1", "z0", "z1", "a0", "a1"]
EXP_UNITS = ["t", "x", "l", "o"] + [f"m{k}" for k in range(NEQ)] + ["e"]
UNIT = {"G": {u: n for n, u in enumerate(GNN_UNITS)}}
UNIT["A"] = UNIT["B"] = UNIT["T"] = {u: n for n, u in enumerate(EXP_UNITS)}
NGNN, NEXP = len(GNN_UNITS), len(EXP_UNITS)


def bank_of(stage, unit, g=None, last=None):
    if stage == "G":
        return int(unit[1]) if isinstance(g, int) and g == 0 else 0
    if isinstance(g, int) and g == last:
        if unit[0] == "m":
            return (1 if stage == "A" else 5) + int(unit[1]) % 2
        return 3 if stage == "A" else 4
    if (stage, unit) == ("A", "o"):
        return 1
    return 1 + int(unit[1]) % 2 if unit[0] == "m" else 0


def bank_before(stage, unit, users, bank, present):
    at = users(0).index((stage, unit))
    for back in range(3):
        for st, u in reversed(users(0)[:at] if back == 0 else users(back)):
            if present(st, back) and bank(st, u, back) == bank(stage, unit, 0):
                return st, u, back
    return None


TAIL = {
    "PE":
        "T:q0 T:q1 T:m3 T:q2 T:m4 A:t T:q3 T:m5 T:q4 T:m6 T:m7 T:q5 A:x T:q6 A:l T:q7 T:e B:t A:o "
        "A:m0 A:m1 A:q0 A:m2 A:q1 B:x A:m3 A:q2 A:m4 B:l A:q3 A:m5 A:m6 A:q4 B:o A:m7 A:q5 B:m0 "
        "A:q6 A:q7 B:m1 A:e B:m2 B:q0 B:m3 B:q1 B:m4 B:q2 B:q3 B:m5 B:m6 B:q4 B:m7 B:q5 B:q6 B:q7 "
        "B:e",
    "ACT":
        "T:m3 T:m4 T:m5 T:m6 A:x T:m7 T:q7 A:o A:m0 A:m1 A:m2 B:x A:m3 A:m4 A:m5 A:m6 B:o A:m7 "
        "A:q7 B:m0 B:m1 B:m2 B:m3 B:m4 B:m5 B:m6 B:m7 B:q7",
    "DVE":
        "T:m3 A:t T:m4 A:u T:m5 A:n T:m6 A:x T:m7 A:l A:k T:e B:t B:u A:m0 A:m1 B:n A:m2 B:x A:m3 "
        "A:m4 B:l B:k A:m5 A:m6 A:m7 B:m0 B:m1 B:m2 A:e B:m3 B:m4 B:m5 B:m6 B:m7 B:e",
}
START = {
    "PE":
        "adj bm0 G:y0 bias ih0 ih1 G:y1 ih2 G:w0 G:w1 ih3 hh1 hh2 G:z0 G:z1 hh3 G:a0 router G:a1",
    "ACT":
        "adj G:c0 wg0 wg1 G:f0 G:c1 G:f1 G:y0 ih0 ih1 G:y1 G:w0 ih2 ih3 G:w1 G:z0 hh1 hh2 hh3 "
        "G:z1 G:a0 G:a1",
    "DVE":
        "G:s0 G:s1 G:s2 G:c0 adj bm0 G:f0 wg0 G:f1 wg1 bsum bias G:y0 ih0 ih1 G:y1 G:w0 G:w1 G:z0 "
        "ih2 ih3 G:z1 hh1 G:a0 hh2 hh3 G:a1",
}
START, TAIL = ({eng: order.split() for eng, order in orders.items()} for orders in (START, TAIL))
TAIL = {eng: [(u[0], u[2:]) for u in order] for eng, order in TAIL.items()}


def bank_users(i, groups):
    if isinstance(i, int) and i == groups:
        units = TAIL["PE"]
    else:
        table = LAST if isinstance(i, int) and i == groups - 1 else FILL
        units = [u for slot in table["PE"] for part in slot for u in part]
    return [(st, u) for st, u in units if u in UNIT[st]]


LATE = {3: ["router"], 4: ["w1"], 5: ["w2"], 6: ["b1", "b2"]}

SETUP = ["adj", "bm0", "wg0", "wg1", "bias"] + [f"ih{p}" for p in range(4)] + \
        [f"hh{p}" for p in range(1, 4)] + ["router", "w1", "w2", "b2"]
N_GNN_LOADS, N_LSTM_LOADS, N_EXPERT_LOADS = 4, 4, 10
LSTM_WEIGHTS = [f"ih{p}" for p in range(4)] + [f"hh{p}" for p in range(1, 4)]
SETUP_AT = {name: n + 1 for n, name in enumerate(SETUP)}
SETUP_PE = ["adj", "bm0", "bias"] + LSTM_WEIGHTS + ["router"]
SETUP_PE_AT = {name: n + 1 for n, name in enumerate(SETUP_PE)}
SETUP_ACT = ["adj", "wg0", "wg1"] + LSTM_WEIGHTS + ["router", "w1", "w2"]
SETUP_ACT_AT = {name: n + 1 for n, name in enumerate(SETUP_ACT)}


def gnn_lstm_moe(nc, x, adj, Wg0, bg0, Wg1, bg1, Wih, Whh, bih, bhh, router_w, router_b, W1, b1, W2, b2, out):
    B, T, D = x.shape
    NG = B // GB
    TOK = GB * T
    KT = T // P
    TILES = TOK // P
    E, _, HE = W1.shape
    EQ = E * HE // P
    EPT = P // HE
    MP = Wih.shape[0]
    assert D == P and KT == 2 and TILES == 8 and EQ == 8 and MP == 4 and TOK == 2 * HALF and E == 32

    ctx = ExitStack()
    with ctx:
        def sb(name, shape, dt=F32):
            return ctx.enter_context(nc.sbuf_tensor(name, shape, dt))

        def sem(name):
            return ctx.enter_context(nc.semaphore(name))

        ident = sb("ident", [P, P])
        ident16 = sb("ident16", [P, P], BF16)
        ones_r = sb("ones_r", [P, P], F32R)
        adjT_hi, adjT_lo = (sb(f"adjT_{v}", [P, KT, T], F32R) for v in ("hi", "lo"))
        wg_hi, wg_lo = (sb(f"wg_{v}", [P, 2, P], F32R) for v in ("hi", "lo"))
        wih_hi, wih_lo = (sb(f"wih_{v}", [P, MP, 4 * P], F32R) for v in ("hi", "lo"))
        whh_hi, whh_lo = (sb(f"whh_{v}", [P, MP - 1, 4 * P], F32R) for v in ("hi", "lo"))
        w1_hi, w1_lo = (sb(f"w1_{v}", [P, E * HE], F32R) for v in ("hi", "lo"))
        w2_hi, w2_lo = (sb(f"w2_{v}", [P, EQ, P], F32R) for v in ("hi", "lo"))
        rT_hi, rT_lo = (sb(f"rT_{v}", [P, E], F32R) for v in ("hi", "lo"))
        wg_raw = sb("wg_raw", [P, 2, P])
        adj_raw = sb("adj_raw", [P, KT, T])
        r_raw = sb("r_raw", [E, P])
        b_raw = sb("b_raw", [4 * MP, 2, P])
        bsum = sb("bsum", [4 * MP, P])
        rb = sb("rb", [P, E])
        bg0col = sb("bg0col", [P, 1])
        bg1row = sb("bg1row", [P, P])
        bm0 = sb("bm0", [P, T])
        gbias = sb("gbias", [P, 4 * MP])
        b1_raw = sb("b1_raw", [3 * E, HE])
        b2_raw = sb("b2_raw", [3 * E, P])
        b1_rest = sb("b1_rest", [3 * E, 2, HE])
        b2_rest = sb("b2_rest", [3 * E, 2, P])
        b1_part = sb("b1_part", [3 * E, 3, HE], BF16)
        b2_part = sb("b2_part", [3 * E, 3, P], BF16)
        b1_sel = sb("b1_sel", [3 * E, EQ, EPT, HE], BF16)
        b2_sel = sb("b2_sel", [3 * E, P], BF16)
        rank = sb("rank", [P, E])
        half_neg = sb("half_neg", [P, TILES])

        pause = sb("pause", [P, 1])

        x_nat = sb("x_nat", [P, TILES, P])
        HT = TILES // 2
        st1 = sb("st1", [P, TILES, 6])
        mv1 = sb("mv1", [P, TILES, 2])
        ve1 = sb("ve1", [P, TILES])
        rs1 = sb("rs1", [P, TILES])
        mrs1 = sb("mrs1", [P, TILES])
        xn = sb("xn", [P, TILES, P])
        xn_hi, xn_lo = (sb(f"xn_{v}", [P, TILES, P], F32R) for v in ("hi", "lo"))
        yz_hi, yz_lo = (sb(f"yz_{v}", [P, 2, HALF], F32R) for v in ("hi", "lo"))
        gf = sb("gf", [P, 2, HALF])
        h1_hi, h1_lo = (sb(f"h1_{v}", [P, 2, HALF], F32R) for v in ("hi", "lo"))
        hin_hi, hin_lo = (sb(f"hin_{v}", [P, TOK], F32R) for v in ("hi", "lo"))
        hb_hi, hb_lo = (sb(f"hb_{v}", [P, T, GB], F32R) for v in ("hi", "lo"))
        gact = sb("gact", [P, 2, 4, HALF])
        cell = sb("cell", [P, HALF])
        ig = sb("ig", [P, HALF])
        fc = sb("fc", [P, HALF])
        tc = sb("tc", [P, HALF])
        hf = sb("hf", [P, HALF])
        hs_hi, hs_lo = (sb(f"hs_{v}", [P, HALF], F32R) for v in ("hi", "lo"))
        hfull = sb("hfull", [P, GB, T])
        x_res = sb("x_res", [P, TILES, P])
        x2 = sb("x2", [P, TILES, P])
        st2 = sb("st2", [P, TILES, 6])
        mv2 = sb("mv2", [P, TILES, 2])
        ve2 = sb("ve2", [P, TILES])
        rs2 = sb("rs2", [P, TILES])
        xn2 = sb("xn2", [P, TILES, P])
        xT_hi, xT_lo = (sb(f"xT_{v}", [P, TOK], F32R) for v in ("hi", "lo"))
        lg = sb("lg", [P, TILES, E])
        lmax = sb("lmax", [P, TILES, 1])
        cand = sb("cand", [P, TILES, E])
        best = sb("best", [P, TILES, 1])
        oh3 = sb("oh3", [P, TILES, 3 * E], BF16)
        ohT = sb("ohT", [3 * E, TOK], BF16)
        hm_hi, hm_lo = (sb(f"hm_{v}", [P, 2, HALF], F32R) for v in ("hi", "lo"))
        orel = sb("orel", [P, HALF])
        obuf = sb("obuf", [P, TILES, P])
        wih_raw = gact[:, 0, :, :].rearrange("p q (r c) -> p (q r) c", c=P)
        whh_raw = gact[:, 1, :, :].rearrange("p q (r c) -> p (q r) c", c=P)
        w1_raw = obuf[:, :, :].rearrange("p a b -> p (a b)")
        w2_raw = xn2

        gate_ps = [ctx.enter_context(nc.psum_tensor(f"gate_ps{q}", [P, HALF], F32)) for q in range(4)]
        fill_ps = [ctx.enter_context(nc.psum_tensor(f"fill_ps{q}", [P, HALF], F32)) for q in range(3)]
        acc_ps = ctx.enter_context(nc.psum_tensor("acc_ps", [P, HALF], F32))
        banks = fill_ps + gate_ps

        adj_loaded, gw_loaded, lw_loaded, ew_loaded = sem("adj_loaded"), sem("gw_loaded"), sem("lw_loaded"), sem("ew_loaded")
        xnat_loaded, xres_loaded = sem("xnat_loaded"), sem("xres_loaded")
        const_made = sem("const_made")
        b1_split = sem("b1_split")
        b1_sel_made = sem("b1_sel_made")
        setup_pe, setup_hi, setup_done = sem("setup_pe"), sem("setup_hi"), sem("setup_done")
        dve_tmp = sem("dve_tmp")
        ln1_stat, ln1_aggr, ln1_var, ln1_rstd = sem("ln1_stat"), sem("ln1_aggr"), sem("ln1_var"), sem("ln1_rstd")
        ln1_shift = sem("ln1_shift")
        ln1_read, ln1_hi, xn_ready = sem("ln1_read"), sem("ln1_hi"), sem("xn_ready")
        gnn_biased, gnn_hi = sem("gnn_biased"), sem("gnn_hi")
        gate_ready, gate_done = sem("gate_ready"), sem("gate_done")
        prod_ready, cell_ready, tanh_ready = sem("prod_ready"), sem("cell_ready"), sem("tanh_ready")
        hf_ready, h_hi_ready, h_lo_ready = sem("hf_ready"), sem("h_hi_ready"), sem("h_lo_ready")
        hfull_ready = sem("hfull_ready")

        def by_half(name):
            a, b = sem(name + "_a"), sem(name + "_b")
            return {"A": a, "B": b, "T": b}

        ready, drained = by_half("ready"), by_half("drained")
        ready["G"], drained["G"] = sem("ready_g"), sem("drained_g")
        ln2_stat, ln2_aggr, ln2_var, ln2_rstd = by_half("ln2_stat"), by_half("ln2_aggr"), by_half("ln2_var"), by_half("ln2_rstd")
        xn2_ready, xT_hi_ready, oh_step = by_half("xn2_ready"), by_half("xT_hi_ready"), by_half("oh_step")
        hm_hi_ready, w2_used = by_half("hm_hi_ready"), by_half("w2_used")
        acc_ready, orel_ready = by_half("acc_ready"), by_half("orel_ready")
        stored = by_half("stored")

        x_v = x.rearrange("(n b) (k s) d -> n s (b k) d", b=GB, s=P)
        out_v = out.rearrange("(n b) (k s) d -> n s (b k) d", b=GB, s=P)

        def columns(n):
            p, s, chunk = STEPS[n]
            return HALF if p == 1 else (T // p) * GB

        def tokens(hi_or_lo, n, last=False):
            p, s, chunk = STEPS[n]
            if p == 1:
                v = hi_or_lo if last is False else hi_or_lo[:, :, :].rearrange("p t b -> p (t b)")
                return v[:, chunk * HALF:(chunk + 1) * HALF]
            a = p - 1 if last else s
            return hi_or_lo[:, a:a + p * (T // p - 1) + 1:p, :]

        def as_tokens(flat, n):
            return flat if STEPS[n][0] == 1 else flat.rearrange("p (t b) -> p t b", b=GB)

        def is_last(n):
            p, s, _ = STEPS[n]
            return s == p - 1

        def wait(eng, s, g, per_group, value):
            if isinstance(g, int):
                if per_group * g + value > 0:
                    eng.wait_ge(s, per_group * g + value)
            else:
                eng.wait_ge(s, g * per_group + value)

        def per_group(stage):
            return NGNN if stage == "G" else NEXP

        def is_ready(eng, stage, g, unit):
            wait(eng, ready[stage], g, per_group(stage), UNIT[stage][unit] + 1)

        def is_drained(eng, stage, g, unit):
            wait(eng, drained[stage], g, per_group(stage), UNIT[stage][unit] + 1)

        def x2_is_taken(eng, g):
            if not (isinstance(g, int) and g < 0):
                is_drained(eng, "A", g, "t")
                is_drained(eng, "B", g, "t")

        def exists(stage, i):
            return not isinstance(i, int) or 0 <= i + STAGE_GROUP[stage] < NG

        def bank_is_free(eng, i, stage, unit):
            at = bank_before(stage, unit, lambda back: bank_users(i - back, NG),
                             lambda st, u, back: bank_of(st, u, i - back + STAGE_GROUP[st], NG - 1),
                             lambda st, back: exists(st, i - back))
            if at is not None:
                st, u, back = at
                is_drained(eng, st, i - back + STAGE_GROUP[st], u)

        def fill(eng, slot, part, i, do):
            table = LAST if isinstance(i, int) and i == NG - 1 else FILL
            for stage, unit in table[eng][slot][part]:
                if exists(stage, i):
                    do(i, stage, i + STAGE_GROUP[stage], unit)

        def start(eng, piece, do):
            for name in START[eng]:
                if name[:2] == "G:":
                    do(-1, "G", 0, name[2:])
                else:
                    piece(name)

        def tail(eng, do):
            for stage, unit in TAIL[eng]:
                do(NG, stage, NG + STAGE_GROUP[stage], unit)

        def half_of(stage):
            return 0 if stage == "A" else 1

        block = ctx.enter_context(nc.Block())

        def run(eng, body):
            for i in range(3):
                body(i)
            with eng.Fori(3, NG - 1) as i:
                body(i)
            body(NG - 1)

        @block.sync
        def _(sp):
            sp.dma_start(adj_raw[:, :, :], adj.rearrange("(k t) s -> t k s", t=P)).then_inc(adj_loaded, 16)
            sp.dma_start(x_nat[:, :, :], x_v[0]).then_inc(xnat_loaded, 16)
            loads = {
                gw_loaded: [
                    (wg_raw[:, 0, :], Wg0), (wg_raw[:, 1, :], Wg1),
                    (bg0col[:, :], bg0.rearrange("(h a) -> h a", a=1)),
                    (bg1row[:, :], bg1.partition_broadcast(P)),
                ],
                lw_loaded: [
                    (b_raw[:, 0, :], bih.rearrange("p (q h) -> (p q) h", h=P)),
                    (b_raw[:, 1, :], bhh.rearrange("p (q h) -> (p q) h", h=P)),
                    (wih_raw, Wih.rearrange("p (q a) h -> a (p q) h", a=P)),
                    (whh_raw, Whh.rearrange("p (q a) h -> a (p q) h", a=P)),
                ],
                ew_loaded: [
                    (r_raw[:, :], router_w), (rb[:, :], router_b.partition_broadcast(P)),
                    (w1_raw.rearrange("p (e h) -> p e h", h=HE), W1.rearrange("e d h -> d e h")),
                    (w2_raw[:, :, :], W2.rearrange("(q e) h d -> (e h) q d", e=EPT)),
                ] + [(b1_raw[E * r:E * r + E, :], b1) for r in range(3)]
                  + [(b2_raw[E * r:E * r + E, :], b2) for r in range(3)],
            }
            for loaded, pairs in loads.items():
                for dst, src in pairs:
                    sp.dma_start(dst, src).then_inc(loaded, 16)
            assert [len(pairs) for pairs in loads.values()] == [N_GNN_LOADS, N_LSTM_LOADS, N_EXPERT_LOADS]

            def body(i):
                if exists("G", i):
                    wait(sp, ln1_read, i + 1, 2, 0)
                    sp.dma_start(x_nat[:, :, :], x_v[i + 1]).then_inc(xnat_loaded, 16)
                if exists("A", i):
                    x2_is_taken(sp, i - 2)
                    sp.dma_start(x_res[:, :, :], x_v[i - 1]).then_inc(xres_loaded, 16)

            run(sp, body)
            body(NG)

        @block.gpsimd
        def _(pool):
            nc.gpsimd.memset(ident[:, :], 0.0).then_inc(const_made, 1)
            nc.gpsimd.memset(ident16[:, :], 0.0).then_inc(const_made, 1)
            nc.gpsimd.memset(ones_r[:, :].bitcast(F32), 1.0).then_inc(const_made, 1)
            nc.gpsimd.memset(half_neg[:, :], -0.5).then_inc(const_made, 1)
            nc.gpsimd.iota(rank[:, :], pattern=[[-1, E]], base=E, channel_multiplier=0,
                           allow_small_or_imprecise_dtypes=True).then_inc(const_made, 1)
            pool.wait_ge(const_made, 5)
            for m in (ident, ident16):
                nc.gpsimd.affine_select(out=m[:, :], in_=m[:, :], compare_op=ALU.not_equal, fill=1.0, base=0,
                                        pattern=[[-1, P]], channel_multiplier=1).then_inc(const_made, 1)

            def power(g, ve, rs, a, b, var, rstd):
                wait(pool, var, g, 1, 1)
                nc.gpsimd.tensor_tensor(rs[:, a:b], ve[:, a:b], half_neg[:, a:b], ALU.pow).then_inc(rstd, 1)

            def unit(i, stage, g, u):
                if (stage, u) == ("G", "s2"):
                    power(g, ve1, rs1, 0, TILES, ln1_var, ln1_rstd)
                elif stage == "G" and u[0] == "f":
                    h = int(u[1])
                    half = slice(h * HT, h * HT + HT)
                    wait(pool, ln1_hi, g, 2, h + 1)
                    nc.gpsimd.tensor_tensor(xn_lo[:, half, :], xn[:, half, :], xn_hi[:, half, :].bitcast(F32),
                                            ALU.subtract).then_inc(xn_ready, 1)
                elif stage in "ABT" and u == "u":
                    a = half_of(stage) * HT
                    power(g, ve2, rs2, a, a + HT, ln2_var[stage], ln2_rstd[stage])
                elif stage in "ABT" and u == "e":
                    is_drained(pool, stage, g, "e")
                    a = half_of(stage) * HT
                    pool.dma_start(out_v[g][:, a:a + HT, :], obuf[:, a:a + HT, :]).then_inc(stored[stage], 16)

            def whole_h(g):
                wait(pool, h_lo_ready, g, NSTEP, NSTEP)
                if not (isinstance(g, int) and g == 0):
                    is_ready(pool, "A", g - 1, "t")
                    is_ready(pool, "B", g - 1, "t")
                for h in range(2):
                    b = slice(h * GB // 2, (h + 1) * GB // 2)
                    o = hfull[:, b, :].rearrange("p b t -> p t b")
                    nc.gpsimd.tensor_tensor(o, hb_hi[:, :, b].bitcast(F32), hb_lo[:, :, b].bitcast(F32), ALU.add)\
                        .then_inc(hfull_ready, 1)

            def selector():
                pool.wait_ge(b1_split, 1)
                pool.wait_ge(xn_ready, 4)
                for r in range(3):
                    if r > 0:
                        pool.wait_ge(b1_sel_made, r)
                    src = b1_part[E * r:E * r + E, r, :].unsqueeze(1).to_broadcast([E, E, HE])
                    nc.gpsimd.affine_select(
                        out=b1_sel[E * r:E * r + E, :, :, :].rearrange("p q e h -> p (q e) h"), in_=src,
                        compare_op=ALU.is_equal, fill=UNPICKED if r == 0 else 0.0, base=0,
                        pattern=[[-1, E], [0, HE]], channel_multiplier=1).then_inc(b1_sel_made, 1)
                pool.wait_ge(b1_sel_made, 3)

            def body(i):
                for n in range(NSTEP):
                    for part in range(2):
                        fill("DVE", n, part, i, unit)
                if isinstance(i, int) and i == 0:
                    selector()
                whole_h(i)

            start("DVE", lambda name: None, unit)
            run(pool, body)
            tail("DVE", unit)
            for stage in "AB":
                pool.wait_ge(stored[stage], 16 * NG)

        @block.tensor
        def _(pe):
            def three(o, w_hi, w_lo, r_hi, r_lo, start, stop):
                nc.tensor.matmul(o, w_hi, r_hi, start=start, stop=False)
                nc.tensor.matmul(o, w_lo, r_hi, start=False, stop=False)
                return nc.tensor.matmul(o, w_hi, r_lo, start=False, stop=stop)

            def piece(name):
                if name == "adj":
                    pe.wait_ge(const_made, 7)
                    pe.wait_ge(adj_loaded, 16)
                    for k in range(KT):
                        for t in range(KT):
                            mm = nc.tensor.transpose(fill_ps[0][:, k * T + t * P:k * T + t * P + P],
                                                     adj_raw[:, t, k * P:k * P + P], ident[:, :])
                elif name == "bm0":
                    pe.wait_ge(setup_done, SETUP_AT["adj"])
                    for k in range(KT):
                        nc.tensor.matmul(fill_ps[2][:, 0:T], ones_r[:, :], adjT_hi[:, k, :], start=(k == 0), stop=False)
                        mm = nc.tensor.matmul(fill_ps[2][:, 0:T], ones_r[:, :], adjT_lo[:, k, :], start=False,
                                              stop=(k == KT - 1))
                elif name == "bias":
                    pe.wait_ge(dve_tmp, 1)
                    mm = nc.tensor.transpose(fill_ps[2][:, T + E:T + E + 4 * MP], bsum[:, :], ident[0:4 * MP, 0:4 * MP])
                elif name == "router":
                    pe.wait_ge(ew_loaded, 16 * N_EXPERT_LOADS)
                    mm = nc.tensor.transpose(fill_ps[2][:, T:T + E], r_raw[:, :], ident[0:E, 0:E])
                else:
                    n, p = LSTM_WEIGHTS.index(name), int(name[2])
                    raw = wih_raw if name[0] == "i" else whh_raw
                    pe.wait_ge(lw_loaded, 16 * N_LSTM_LOADS)
                    if n >= 4:
                        pe.wait_ge(setup_done, SETUP_AT[LSTM_WEIGHTS[n - 4]])
                    for q in range(4):
                        mm = nc.tensor.transpose(gate_ps[n % 4][:, q * P:q * P + P], raw[:, 4 * p + q, :], ident[:, :])
                mm.then_inc(setup_pe, 1)

            def gnn(i, g, unit):
                kind, u = unit[0], int(unit[1])
                bank_is_free(pe, i, "G", unit)
                bank = banks[bank_of("G", unit, g)]
                if kind == "w" and isinstance(g, int) and g == 0:
                    pe.wait_ge(setup_done, SETUP_AT["wg1"])
                if kind == "y":
                    wait(pe, xn_ready, g, 2, u + 1)
                    for bb in range(2):
                        o = bank[:, bb * T:bb * T + T]
                        for k in range(KT):
                            j = (2 * u + bb) * KT + k
                            mm = three(o, xn_hi[:, j, :], xn_lo[:, j, :], adjT_hi[:, k, :], adjT_lo[:, k, :],
                                       k == 0, k == KT - 1)
                elif kind == "w":
                    is_drained(pe, "G", g, f"y{u}")
                    mm = three(bank[:, :], wg_hi[:, 0, :], wg_lo[:, 0, :], yz_hi[:, u, :], yz_lo[:, u, :], True, True)
                elif kind == "z":
                    is_drained(pe, "G", g, f"w{u}")
                    for j in range(2 * KT):
                        c = slice(j * P, j * P + P)
                        mm = three(bank[:, c], h1_hi[:, u, c], h1_lo[:, u, c], wg_hi[:, 1, :], wg_lo[:, 1, :],
                                   True, True)
                else:
                    is_drained(pe, "G", g, f"z{u}")
                    for bb in range(2):
                        o = bank[:, bb * T:bb * T + T]
                        for k in range(KT):
                            c = slice((bb * KT + k) * P, (bb * KT + k) * P + P)
                            mm = three(o, yz_hi[:, u, c], yz_lo[:, u, c], adjT_hi[:, k, :], adjT_lo[:, k, :],
                                       k == 0, k == KT - 1)
                mm.then_inc(ready["G"], 1)

            def early_gates(n):
                p, s, _ = STEPS[n]
                return (I_, G_) if s > 0 or p > 1 else ()

            def gates_x(g, n):
                p, s, _ = STEPS[n]
                N = columns(n)
                if p == 1:
                    is_drained(pe, "G", g, "a1")
                    r_hi, r_lo = tokens(hin_hi, n), tokens(hin_lo, n)
                else:
                    r_hi, r_lo = tokens(hb_hi, n), tokens(hb_lo, n)
                    if s == 0:
                        wait(pe, h_hi_ready, g, NSTEP, n)
                early = early_gates(n) if s == 0 else ()
                for q in gates_of(s):
                    back, t = tile_before(n, q)
                    wait(pe, gate_done, g, NTILE, t + 1 - back * NTILE)
                    o, c = as_tokens(gate_ps[q][:, 0:N], n), slice(q * P, q * P + P)
                    if q in early:
                        nc.tensor.matmul(o, wih_hi[:, p - 1, c], r_hi, start=True, stop=False)
                        nc.tensor.matmul(o, wih_lo[:, p - 1, c], r_hi, start=False, stop=False)
                        if q == early[-1]:
                            wait(pe, h_lo_ready, g, NSTEP, n)
                            for e in early:
                                nc.tensor.matmul(as_tokens(gate_ps[e][:, 0:N], n), wih_hi[:, p - 1, e * P:e * P + P],
                                                 r_lo, start=False, stop=True).then_inc(gate_ready, 1)
                    else:
                        mm = three(o, wih_hi[:, p - 1, c], wih_lo[:, p - 1, c], r_hi, r_lo, True, s == 0)
                        if s == 0:
                            mm.then_inc(gate_ready, 1)

            def gates_h(g, n):
                p, s, _ = STEPS[n]
                N = columns(n)
                wait(pe, h_hi_ready, g, NSTEP, n)
                early = early_gates(n)
                for q in gates_of(s):
                    o, c = gate_ps[q][:, 0:N], slice(q * P, q * P + P)
                    nc.tensor.matmul(o, whh_hi[:, p - 2, c], hs_hi[:, 0:N], start=False, stop=False)
                    nc.tensor.matmul(o, whh_lo[:, p - 2, c], hs_hi[:, 0:N], start=False, stop=False)
                    if q == early[-1]:
                        wait(pe, h_lo_ready, g, NSTEP, n)
                    for e in (early if q == early[-1] else () if q in early else (q,)):
                        nc.tensor.matmul(gate_ps[e][:, 0:N], whh_hi[:, p - 2, e * P:e * P + P], hs_lo[:, 0:N],
                                         start=False, stop=True).then_inc(gate_ready, 1)

            def second_product(stage, g, q):
                if q == 0:
                    if stage == "A":
                        if not (isinstance(g, int) and g == 0):
                            wait(pe, orel_ready["B"], g, 1, 0)
                    else:
                        wait(pe, orel_ready["A"], g, 1, 1)
                is_drained(pe, stage, g, f"m{q}")
                three(acc_ps[:, :], w2_hi[:, q, :], w2_lo[:, q, :], hm_hi[:, q % 2, :], hm_lo[:, q % 2, :],
                      q == 0, False).then_inc(w2_used[stage], 1)
                if q == EQ - 1:
                    c = slice(half_of(stage) * HALF, half_of(stage) * HALF + HALF)
                    nc.tensor.matmul(acc_ps[:, :], b2_sel[:, :], ohT[:, c], start=False, stop=True)\
                        .then_inc(acc_ready[stage], 1)

            def expert(i, stage, g, unit):
                if unit[0] == "q":
                    second_product(stage, g, int(unit[1]))
                    return
                h = half_of(stage)
                o = banks[bank_of(stage, unit, g, NG - 1)]
                c = slice(h * HALF, h * HALF + HALF)
                bank_is_free(pe, i, stage, unit)
                if unit == "t":
                    wait(pe, hfull_ready, g, 2, h + 1)
                    cols = hfull[:, :, :].rearrange("p b t -> p (b t)")
                    for j in range(HT):
                        at = (HT * h + j) * P
                        mm = nc.tensor.transpose(o[:, j * P:j * P + P], cols[:, at:at + P], ident[:, :])
                elif unit == "x":
                    wait(pe, xn2_ready[stage], g, 1, 1)
                    for j in range(HT):
                        mm = nc.tensor.transpose(o[:, j * P:j * P + P], xn2[:, HT * h + j, :], ident[:, :])
                elif unit == "l":
                    if stage == "A" and isinstance(g, int) and g == 0:
                        pe.wait_ge(setup_done, SETUP_AT["b2"])
                    is_drained(pe, stage, g, "x")
                    for j in range(HT):
                        t = slice(h * HALF + j * P, h * HALF + j * P + P)
                        mm = three(o[:, j * E:j * E + E], xT_hi[:, t], xT_lo[:, t], rT_hi[:, :], rT_lo[:, :], True, True)
                elif unit == "o":
                    wait(pe, oh_step[stage], g, 7, 7)
                    o16 = o[:, :].bitcast(BF16)
                    for j in range(HT):
                        mm = nc.tensor.transpose(o16[0:3 * E, j * P:j * P + P], oh3[:, HT * h + j, :], ident16[:, :])
                elif unit[0] == "m":
                    q = int(unit[1])
                    if q == 0:
                        is_drained(pe, stage, g, "o")
                        if stage == "A" and isinstance(g, int) and g == 0:
                            pe.wait_ge(b1_sel_made, 3)
                    nc.tensor.matmul(o[:, :], b1_sel[:, q, :, :].rearrange("p e h -> p (e h)"), ohT[:, c],
                                     start=True, stop=False)
                    mm = three(o[:, :], w1_hi[:, q * P:q * P + P], w1_lo[:, q * P:q * P + P], xT_hi[:, c], xT_lo[:, c],
                               False, True)
                else:
                    wait(pe, orel_ready[stage], g, 1, 1)
                    for j in range(HT):
                        mm = nc.tensor.transpose(o[:, j * P:j * P + P], orel[:, j * P:j * P + P], ident[:, :])
                mm.then_inc(ready[stage], 1)

            def unit(i, stage, g, u):
                if stage == "G":
                    gnn(i, g, u)
                else:
                    expert(i, stage, g, u)

            def body(i):
                if isinstance(i, int) and i == 0:
                    pe.wait_ge(setup_done, SETUP_AT["hh3"])
                for n in range(NSTEP):
                    if STEPS[n][1] == 0:
                        gates_x(i, n)
                    else:
                        gates_h(i, n)
                    fill("PE", n, 0, i, unit)
                    if n + 1 < NSTEP and STEPS[n + 1][1] > 0:
                        gates_x(i, n + 1)
                    fill("PE", n, 1, i, unit)

            start("PE", piece, unit)
            run(pe, body)
            tail("PE", unit)

        @block.scalar
        def _(act):
            def hi_of(dst, src):
                return nc.scalar.copy(dst, src)

            def piece(name):
                if name == "adj":
                    act.wait_ge(setup_pe, SETUP_PE_AT["adj"])
                    a = hi_of(adjT_hi[:, :, :].rearrange("p k t -> p (k t)"), fill_ps[0][:, :])
                elif name[:2] == "wg":
                    n = int(name[2])
                    act.wait_ge(gw_loaded, 16 * N_GNN_LOADS)
                    a = hi_of(wg_hi[:, n, :], wg_raw[:, n, :])
                elif name in LSTM_WEIGHTS:
                    n = LSTM_WEIGHTS.index(name)
                    act.wait_ge(setup_pe, SETUP_PE_AT[name])
                    a = hi_of(wih_hi[:, n, :] if n < 4 else whh_hi[:, n - 4, :], gate_ps[n % 4][:, :])
                elif name == "router":
                    act.wait_ge(setup_pe, SETUP_PE_AT["router"])
                    a = hi_of(rT_hi[:, :], fill_ps[2][:, T:T + E])
                else:
                    act.wait_ge(ew_loaded, 16 * N_EXPERT_LOADS)
                    if name == "w1":
                        a = hi_of(w1_hi[:, :], w1_raw)
                    else:
                        a = hi_of(w2_hi[:, :, :], w2_raw[:, :, :])
                a.then_inc(setup_hi, 1)

            def gnn(g, unit):
                half = range(int(unit[1]) * HT, int(unit[1]) * HT + HT)
                if unit[0] == "c":
                    if not (isinstance(g, int) and g == 0):
                        is_drained(act, "G", g - 1, "y1")
                    wait(act, ln1_shift, g, 1, 1)
                    for j in half:
                        a = nc.scalar.activation(xn[:, j, :], x_nat[:, j, :], ACT.Identity, bias=mrs1[:, j:j + 1],
                                                 scale=rs1[:, j:j + 1])
                    a.then_inc(ln1_read, 1)
                    return
                if unit[0] == "f":
                    wait(act, ln1_read, g, 2, int(unit[1]) + 1)
                    hi_of(xn_hi[:, half.start:half.stop, :], xn[:, half.start:half.stop, :]).then_inc(ln1_hi, 1)
                    return
                kind, u, n = unit[0], int(unit[1]), UNIT["G"][unit]
                if kind in "wz":
                    wait(act, gnn_biased, g, 4, n - 1)
                    if kind == "w":
                        a = nc.scalar.activation(h1_hi[:, u, :], gf[:, u, :], ACT.Relu)
                    else:
                        a = hi_of(yz_hi[:, u, :], gf[:, u, :])
                else:
                    is_ready(act, "G", g, unit)
                    if kind == "y":
                        a = hi_of(yz_hi[:, u, :], banks[bank_of("G", unit, g)][:, :])
                    else:
                        o = hin_hi[:, :].rearrange("p (t b) -> p b t", b=GB)[:, 2 * u:2 * u + 2, :]
                        a = nc.scalar.activation(o, banks[bank_of("G", unit, g)][:, :].rearrange("p (b t) -> p b t", b=2), ACT.Relu)
                a.then_inc(gnn_hi, 1)

            def gates(g, n):
                p, s, _ = STEPS[n]
                N = columns(n)
                if n == 0:
                    wait(act, h_hi_ready, g, NSTEP, 0)
                for q in gates_of(s):
                    wait(act, gate_ready, g, NTILE, TILE[n, q] + 1)
                    nc.scalar.activation(gact[:, n % 2, q, 0:N], gate_ps[q][:, 0:N], ACT.Tanh if q == G_ else ACT.Sigmoid,
                                         bias=gbias[:, 4 * (p - 1) + q:4 * (p - 1) + q + 1]).then_inc(gate_done, 1)

            def cell_tanh(g, n):
                N = columns(n)
                wait(act, cell_ready, g, NSTEP, n + 1)
                nc.scalar.activation(tc[:, 0:N], cell[:, 0:N], ACT.Tanh).then_inc(tanh_ready, 1)

            def expert(stage, g, unit):
                h = half_of(stage)
                c = slice(h * HALF, h * HALF + HALF)
                o = banks[bank_of(stage, unit, g, NG - 1)]
                if unit == "x":
                    is_ready(act, stage, g, unit)
                    hi_of(xT_hi[:, c], o[:, :]).then_inc(xT_hi_ready[stage], 1)
                elif unit == "o":
                    is_ready(act, stage, g, unit)
                    nc.scalar.copy(ohT[:, c], o[:, :].bitcast(BF16)[0:3 * E, 0:HALF]).then_inc(drained[stage], 1)
                elif unit[0] == "m":
                    q = int(unit[1])
                    if q > 1:
                        wait(act, w2_used[stage], g, EQ, q - 1)
                    is_ready(act, stage, g, unit)
                    nc.scalar.activation(hm_hi[:, q % 2, :], o[:, :], ACT.Relu).then_inc(hm_hi_ready[stage], 1)
                elif unit == "q7":
                    wait(act, acc_ready[stage], g, 1, 1)
                    nc.scalar.activation(orel[:, :], acc_ps[:, :], ACT.Relu).then_inc(orel_ready[stage], 1)

            def unit(i, stage, g, u):
                if stage == "G":
                    gnn(g, u)
                else:
                    expert(stage, g, u)

            def body(i):
                for n in range(NSTEP):
                    gates(i, n)
                    fill("ACT", n, 0, i, unit)
                    cell_tanh(i, n)
                    fill("ACT", n, 1, i, unit)
                    if isinstance(i, int) and i == 0:
                        for name in LATE.get(n, []):
                            if name in SETUP_ACT:
                                piece(name)

            start("ACT", piece, unit)
            act.wait_ge(setup_done, SETUP_AT["bias"])
            run(act, body)
            tail("ACT", unit)

        @block.vector
        def _(dve):
            links = [0]

            def link(ins):
                links[0] += 1
                ins.then_inc(dve_tmp, 1)
                dve.wait_ge(dve_tmp, links[0])

            def lo_of(dst, src, hi, op0=ALU.max, scalar=None):
                if scalar is None:
                    return nc.vector.tensor_tensor(dst, src, hi.bitcast(F32), ALU.subtract)
                return nc.vector.scalar_tensor_tensor(out=dst, in0=src, scalar=scalar, in1=hi.bitcast(F32), op0=op0,
                                                      op1=ALU.subtract)

            def statistics(src, st, a, b):
                for j in range(a, b):
                    last = nc.vector.bn_stats(st[:, j, :], src[:, j, :])
                return last

            def moments(g, st, mv, ve, a, b, stat, aggr, var):
                wait(dve, stat, g, 1, 1)
                nc.vector.memset(pause[:, :], 0.0)
                for j in range(a, b):
                    last = nc.vector.bn_aggr(mv[:, j, :], st[:, j, :])
                last.then_inc(aggr, 1)
                wait(dve, aggr, g, 1, 1)
                nc.vector.tensor_scalar(ve[:, a:b], mv[:, a:b, 1], EPS, None, ALU.add).then_inc(var, 1)

            def gnn(g, unit):
                if unit[0] == "f":
                    return
                if unit == "c0":
                    wait(dve, ln1_rstd, g, 1, 1)
                    nc.vector.scalar_tensor_tensor(out=mrs1[:, :], in0=mv1[:, :, 0], scalar=-1.0, in1=rs1[:, :],
                                                   op0=ALU.mult, op1=ALU.mult).then_inc(ln1_shift, 1)
                    return
                if unit == "s1":
                    statistics(x_nat, st1, HT, TILES).then_inc(ln1_stat, 1)
                    return
                if unit == "s2":
                    moments(g, st1, mv1, ve1, 0, TILES, ln1_stat, ln1_aggr, ln1_var)
                    return
                if unit == "s0":
                    wait(dve, xnat_loaded, g, 16, 16)
                    wait(dve, ln1_read, g, 2, 0)
                    statistics(x_nat, st1, 0, HT)
                    return
                kind, u, n = unit[0], int(unit[1]), UNIT["G"][unit]
                o = banks[bank_of("G", unit, g)]
                if kind in "wz":
                    is_ready(dve, "G", g, unit)
                    if kind == "w":
                        bias, shape = bm0[:, :], [P, 2, T]
                    else:
                        bias, shape = bg1row[:, :], [P, 2 * KT, P]
                    view = lambda v: v.rearrange("p (a b) -> p a b", a=shape[1])
                    nc.vector.tensor_tensor(view(gf[:, u, :]), view(o[:, :]), bias.unsqueeze(1).to_broadcast(shape),
                                            ALU.add).then_inc(gnn_biased, 1)
                    wait(dve, gnn_hi, g, NGNN, n + 1)
                    if kind == "w":
                        a = lo_of(h1_lo[:, u, :], gf[:, u, :], h1_hi[:, u, :], scalar=0.0)
                    else:
                        a = lo_of(yz_lo[:, u, :], gf[:, u, :], yz_hi[:, u, :])
                else:
                    wait(dve, gnn_hi, g, NGNN, n + 1)
                    if kind == "y":
                        a = lo_of(yz_lo[:, u, :], o[:, :], yz_hi[:, u, :])
                    else:
                        tb = lambda v: v[:, :].rearrange("p (t b) -> p b t", b=GB)[:, 2 * u:2 * u + 2, :]
                        a = lo_of(tb(hin_lo), o[:, :].rearrange("p (b t) -> p b t", b=2), tb(hin_hi), scalar=0.0)
                a.then_inc(drained["G"], 1)

            def new_cell(g, n):
                p, s, _ = STEPS[n]
                N = columns(n)
                gate = lambda q: gact[:, n % 2, q, 0:N]
                done = lambda q: wait(dve, gate_done, g, NTILE, TILE[n, q] + 1)
                done(G_)
                if s == 0:
                    nc.vector.tensor_tensor(cell[:, 0:N], gate(I_), gate(G_), ALU.mult).then_inc(cell_ready, 1)
                else:
                    nc.vector.tensor_tensor(ig[:, 0:N], gate(I_), gate(G_), ALU.mult).then_inc(prod_ready, 1)
                    done(F_)
                    nc.vector.tensor_tensor(fc[:, 0:N], gate(F_), cell[:, 0:N], ALU.mult).then_inc(prod_ready, 1)
                    later = [m for m in range(NSTEP) if STEPS[m][1] > 0]
                    wait(dve, prod_ready, g, 2 * len(later), 2 * later.index(n) + 2)
                    nc.vector.tensor_tensor(cell[:, 0:N], ig[:, 0:N], fc[:, 0:N], ALU.add).then_inc(cell_ready, 1)

            def new_h(g, n):
                N = columns(n)
                wait(dve, gate_done, g, NTILE, TILE[n, O_] + 1)
                wait(dve, tanh_ready, g, NSTEP, n + 1)
                if n == 0:
                    wait(dve, hfull_ready, g, 2, 0)
                nc.vector.tensor_tensor(hf[:, 0:N], gact[:, n % 2, O_, 0:N], tc[:, 0:N], ALU.mult).then_inc(hf_ready, 1)
                wait(dve, hf_ready, g, NSTEP, n + 1)
                if is_last(n):
                    hi, lo = tokens(hb_hi, n, last=True), tokens(hb_lo, n, last=True)
                    src = as_tokens(hf[:, 0:N], n)
                else:
                    hi, lo, src = hs_hi[:, 0:N], hs_lo[:, 0:N], hf[:, 0:N]
                nc.vector.tensor_copy(hi, src).then_inc(h_hi_ready, 1)
                wait(dve, h_hi_ready, g, NSTEP, n + 1)
                lo_of(lo, src, hi).then_inc(h_lo_ready, 1)

            def expert(stage, g, unit):
                h = half_of(stage)
                a, b = h * HT, h * HT + HT
                c = slice(h * HALF, h * HALF + HALF)
                o = banks[bank_of(stage, unit, g, NG - 1)]
                by_tile = o[:, :].rearrange("p (a b) -> p a b", b=P)
                if unit == "t":
                    wait(dve, xres_loaded, g, 16, 16)
                    wait(dve, drained[stage], g, NEXP, 0)
                    is_ready(dve, stage, g, unit)
                    nc.vector.tensor_tensor(x2[:, a:b, :], by_tile, x_res[:, a:b, :], ALU.add).then_inc(drained[stage], 1)
                elif unit == "u":
                    is_drained(dve, stage, g, "t")
                    statistics(x2, st2, a, b).then_inc(ln2_stat[stage], 1)
                    moments(g, st2, mv2, ve2, a, b, ln2_stat[stage], ln2_aggr[stage], ln2_var[stage])
                elif unit == "n":
                    wait(dve, ln2_rstd[stage], g, 1, 1)
                    for j in range(a, b):
                        last = nc.vector.tensor_scalar(xn2[:, j, :], x2[:, j, :], mv2[:, j, 0:1], rs2[:, j:j + 1],
                                                       ALU.subtract, ALU.mult)
                    last.then_inc(xn2_ready[stage], 1)
                elif unit == "x":
                    wait(dve, xT_hi_ready[stage], g, 1, 1)
                    lo_of(xT_lo[:, c], o[:, :], xT_hi[:, c]).then_inc(drained[stage], 1)
                elif unit in "lk":
                    full = [P, HT, E]
                    L, C, M, X = lg[:, a:b, :], cand[:, a:b, :], lmax[:, a:b, :], best[:, a:b, :]
                    step = lambda ins: ins.then_inc(oh_step[stage], 1)
                    if unit == "l":
                        is_ready(dve, stage, g, unit)
                        logits = o[:, 0:HT * E].rearrange("p (a b) -> p a b", b=E)
                        nc.vector.tensor_tensor(L, logits, rb[:, :].unsqueeze(1).to_broadcast(full), ALU.add)\
                            .then_inc(drained[stage], 1)
                        is_drained(dve, stage, g, unit)
                        step(nc.vector.tensor_reduce(M[:, :, 0], L, AX.X, ALU.max))
                        wait(dve, oh_step[stage], g, 7, 1)
                        step(nc.vector.tensor_tensor(C, L, M.to_broadcast(full), ALU.is_ge))
                        return
                    wait(dve, oh_step[stage], g, 7, 2)
                    step(nc.vector.tensor_tensor(C, C, rank[:, :].unsqueeze(1).to_broadcast(full), ALU.mult))
                    wait(dve, oh_step[stage], g, 7, 3)
                    step(nc.vector.tensor_reduce(X[:, :, 0], C, AX.X, ALU.max))
                    wait(dve, oh_step[stage], g, 7, 4)
                    for r in range(3):
                        step(nc.vector.tensor_tensor(oh3[:, a:b, r * E:r * E + E], C, X.to_broadcast(full), ALU.is_equal))
                elif unit[0] == "m":
                    q = int(unit[1])
                    wait(dve, hm_hi_ready[stage], g, EQ, q + 1)
                    lo_of(hm_lo[:, q % 2, :], o[:, :], hm_hi[:, q % 2, :], scalar=0.0).then_inc(drained[stage], 1)
                elif unit == "e":
                    is_ready(dve, stage, g, unit)
                    wait(dve, stored[stage], g, 16, 0)
                    nc.vector.tensor_tensor(obuf[:, a:b, :], by_tile, x2[:, a:b, :], ALU.add).then_inc(drained[stage], 1)

            def unit(i, stage, g, u):
                if stage == "G":
                    gnn(g, u)
                else:
                    expert(stage, g, u)

            def parts_of(raw, rest, part):
                src = raw[:, :]
                for r in range(3):
                    link(nc.vector.tensor_copy(part[:, r, :], src))
                    if r < 2:
                        link(nc.vector.tensor_tensor(rest[:, r, :], src, part[:, r, :], ALU.subtract))
                        src = rest[:, r, :]

            def piece(name):
                if name in SETUP_ACT:
                    dve.wait_ge(setup_hi, SETUP_ACT_AT[name])
                if name == "adj":
                    a = lo_of(adjT_lo[:, :, :].rearrange("p k t -> p (k t)"), fill_ps[0][:, :],
                              adjT_hi[:, :, :].rearrange("p k t -> p (k t)"))
                elif name == "bsum":
                    dve.wait_ge(lw_loaded, 16 * N_LSTM_LOADS)
                    link(nc.vector.tensor_tensor(bsum[:, :], b_raw[:, 0, :], b_raw[:, 1, :], ALU.add))
                    return
                elif name == "bm0":
                    dve.wait_ge(gw_loaded, 16 * N_GNN_LOADS)
                    dve.wait_ge(setup_pe, SETUP_PE_AT["bm0"])
                    a = nc.vector.tensor_scalar(bm0[:, :], fill_ps[2][:, 0:T], bg0col[:, 0:1], None, ALU.mult)
                elif name[:2] == "wg":
                    n = int(name[2])
                    a = lo_of(wg_lo[:, n, :], wg_raw[:, n, :], wg_hi[:, n, :])
                elif name == "bias":
                    dve.wait_ge(setup_pe, SETUP_PE_AT["bias"])
                    a = nc.vector.tensor_copy(gbias[:, :], fill_ps[2][:, T + E:T + E + 4 * MP])
                elif name in LSTM_WEIGHTS:
                    n = LSTM_WEIGHTS.index(name)
                    hi, lo = (wih_hi[:, n, :], wih_lo[:, n, :]) if n < 4 else (whh_hi[:, n - 4, :], whh_lo[:, n - 4, :])
                    a = lo_of(lo, gate_ps[n % 4][:, :], hi)
                elif name == "router":
                    a = lo_of(rT_lo[:, :], fill_ps[2][:, T:T + E], rT_hi[:, :])
                elif name == "w1":
                    a = lo_of(w1_lo[:, :], w1_raw, w1_hi[:, :])
                elif name == "w2":
                    a = lo_of(w2_lo[:, :, :], w2_raw[:, :, :], w2_hi[:, :, :])
                elif name == "b1":
                    parts_of(b1_raw, b1_rest, b1_part)
                    nc.vector.engine_nop().then_inc(b1_split, 1)
                    return
                else:
                    parts_of(b2_raw, b2_rest, b2_part)
                    for r in range(3):
                        a = nc.vector.tensor_copy(b2_sel[E * r:E * r + E, :], b2_part[E * r:E * r + E, r, :])
                a.then_inc(setup_done, 1)

            def body(i):
                for n in range(NSTEP):
                    new_cell(i, n)
                    fill("DVE", n, 0, i, unit)
                    new_h(i, n)
                    fill("DVE", n, 1, i, unit)
                    if isinstance(i, int) and i == 0:
                        for name in LATE.get(n, []):
                            piece(name)

            start("DVE", piece, unit)
            run(dve, body)
            tail("DVE", unit)



_INS = ["x", "adj", "L0_gnn_Wg0", "L0_gnn_bg0", "L0_gnn_Wg1", "L0_gnn_bg1", "L0_gnn_Wih", "L0_gnn_Whh", "L0_gnn_bih",
        "L0_gnn_bhh", "L0_ffn_router_w", "L0_ffn_router_b", "L0_ffn_W1", "L0_ffn_b1", "L0_ffn_W2", "L0_ffn_b2"]


def kernel(**inputs):
    import numpy as _np
    import concourse.bacc as _bacc
    from concourse import mybir as _mybir
    from concourse.bass_utils import run_bass_kernel_spmd as _run

    nc = _bacc.Bacc("TRN2", target_bir_lowering=False, num_devices=1)
    arrays, args = {}, []
    for name in _INS:
        a = _np.ascontiguousarray(inputs[name])
        arrays[f"in_{name}_dram"] = a
        args.append(nc.dram_tensor(f"in_{name}_dram", a.shape, _mybir.dt.from_np(a.dtype), kind="ExternalInput").ap())
    shape = arrays["in_x_dram"].shape
    args.append(nc.dram_tensor("out_0_dram", shape, _mybir.dt.float32, kind="ExternalOutput").ap())
    gnn_lstm_moe(nc, *args)
    r = _run(nc, [arrays], core_ids=[0])
    return r.results[0]["out_0_dram"]
```
